# Optimizing a Trainium2 kernel written in Bass

```python
import numpy as np
import jax
import jax.numpy as jnp

def _softmax(x, axis=-1):
    return jax.nn.softmax(x, axis=axis)

def _gelu(x):
    return jax.nn.gelu(x, approximate=True)

def _silu(x):
    return jax.nn.silu(x)

def _sigmoid(x):
    return jax.nn.sigmoid(x)

def _layernorm(x, axis=-1, eps=1e-05):
    m = jnp.mean(x, axis=axis, keepdims=True)
    v = jnp.var(x, axis=axis, keepdims=True)
    return (x - m) / jnp.sqrt(v + eps)

def _scatter_add(tgt, idx, src, axis=0):
    return tgt.at[idx].add(src)

def _segment_sum(src, seg, n):
    return jax.ops.segment_sum(src, seg, n)
kernel_name = 'mk_seq_preln_d1_jaxref_r4_332231'

def setup_inputs(seed: int=0):
    np.random.seed(seed)
    _w = jnp.asarray

    def _L0_attn_setup():
        import jax, jax.numpy as jnp
        import numpy as np
        B, S, QD = (2, 1024, 512)
        H, D = (32, 64)
        INNER = H * D
        key = jax.random.key(seed)
        ks = jax.random.split(key, 6)
        scale = 1.0 / np.sqrt(QD)
        return {'hidden_states': jax.random.normal(ks[0], (B, S, QD), dtype=jnp.float32), 'Wq': jax.random.normal(ks[1], (QD, INNER), dtype=jnp.float32) * scale, 'Wk': jax.random.normal(ks[2], (QD, INNER), dtype=jnp.float32) * scale, 'Wv': jax.random.normal(ks[3], (QD, INNER), dtype=jnp.float32) * scale, 'Wo': jax.random.normal(ks[4], (INNER, QD), dtype=jnp.float32) * (1.0 / np.sqrt(INNER)), 'bo': jax.random.normal(ks[5], (QD,), dtype=jnp.float32) * 0.01}
    _L0_attn_in = _L0_attn_setup()

    def _L0_ffn_setup():
        import jax, jax.numpy as jnp
        import numpy as np
        E, TOP_K, D, H = (8, 2, 512, 352)
        B, S = (2, 512)
        key = jax.random.key(seed)
        ks = jax.random.split(key, 8)
        x = jax.random.normal(ks[0], (B, S, D), dtype=jnp.float32)
        gate_w = jax.random.normal(ks[1], (E, D), dtype=jnp.float32) * (1.0 / np.sqrt(D))
        gate_b = jax.random.normal(ks[2], (E,), dtype=jnp.float32) * 0.01
        bias = jnp.zeros((E,), dtype=jnp.float32)
        w1 = jax.random.normal(ks[3], (E, H, D), dtype=jnp.float32) * (1.0 / np.sqrt(D))
        b1 = jax.random.normal(ks[4], (E, H), dtype=jnp.float32) * 0.01
        w2 = jax.random.normal(ks[5], (E, D, H), dtype=jnp.float32) * (1.0 / np.sqrt(H))
        b2 = jax.random.normal(ks[6], (E, D), dtype=jnp.float32) * 0.01
        return {'x': x, 'gate_w': gate_w, 'gate_b': gate_b, 'bias': bias, 'w1': w1, 'b1': b1, 'w2': w2, 'b2': b2}
    _L0_ffn_in = _L0_ffn_setup()
    _d = {'L0_attn_hidden_states': _L0_attn_in['hidden_states'], 'L0_attn_Wq': _L0_attn_in['Wq'], 'L0_attn_Wk': _L0_attn_in['Wk'], 'L0_attn_Wv': _L0_attn_in['Wv'], 'L0_attn_Wo': _L0_attn_in['Wo'], 'L0_attn_bo': _L0_attn_in['bo'], 'L0_ffn_gate_w': _L0_ffn_in['gate_w'], 'L0_ffn_gate_b': _L0_ffn_in['gate_b'], 'L0_ffn_bias': _L0_ffn_in['bias'], 'L0_ffn_w1': _L0_ffn_in['w1'], 'L0_ffn_b1': _L0_ffn_in['b1'], 'L0_ffn_w2': _L0_ffn_in['w2'], 'L0_ffn_b2': _L0_ffn_in['b2']}
    _x0 = _d['L0_attn_hidden_states']
    _d['L0_attn_hidden_states'] = jax.random.normal(jax.random.fold_in(jax.random.key(seed), 1), (1, 2048, 512), dtype=_x0.dtype)
    del _x0
    return _d

def reference(L0_attn_hidden_states, L0_attn_Wq, L0_attn_Wk, L0_attn_Wv, L0_attn_Wo, L0_attn_bo, L0_ffn_gate_w, L0_ffn_gate_b, L0_ffn_bias, L0_ffn_w1, L0_ffn_b1, L0_ffn_w2, L0_ffn_b2):

    def _L0_attn_ref(hidden_states, Wq, Wk, Wv, Wo, bo):
        import jax, jax.numpy as jnp
        import numpy as np
        B, S, QD = (2, 1024, 512)
        H, D = (32, 64)
        INNER = H * D
        b, s, _ = hidden_states.shape

        def proj(W):
            return (hidden_states @ W).reshape(b, s, H, D).transpose(0, 2, 1, 3)
        q = jax.nn.relu(proj(Wq))
        k = jax.nn.relu(proj(Wk))
        v = proj(Wv)
        kv = jnp.einsum('bhsd,bhse->bhde', k, v)
        qkv = jnp.einsum('bhsd,bhde->bhse', q, kv)
        key_sum = k.sum(axis=2)
        normalizer = jnp.einsum('bhsd,bhd->bhs', q, key_sum)
        normalizer = jnp.clip(normalizer, 1e-06, None)[..., None]
        out = qkv / normalizer
        out = out.transpose(0, 2, 1, 3).reshape(b, s, INNER)
        return out @ Wo + bo

    def _L0_ffn_ref(x, gate_w, gate_b, bias, w1, b1, w2, b2):
        import jax, jax.numpy as jnp
        import numpy as np
        E, TOP_K, D, H = (8, 2, 512, 352)
        B, S = (2, 512)
        b, s, d = x.shape
        xf = x.reshape(-1, d)
        scores = xf @ gate_w.T + gate_b + bias
        top_scores, top_idx = jax.lax.top_k(scores, TOP_K)
        gates = jax.nn.softmax(top_scores, axis=-1)
        comb = jnp.sum(jax.nn.one_hot(top_idx, E, dtype=gates.dtype) * gates[..., None], axis=1)
        h = jax.nn.silu(jnp.einsum('td,ehd->teh', xf, w1) + b1)
        y = jnp.einsum('teh,edh->ted', h, w2) + b2
        out = jnp.einsum('ted,te->td', y, comb)
        return out.reshape(b, s, d)
    x = L0_attn_hidden_states
    x = x + _L0_attn_ref(_layernorm(x, axis=-1), L0_attn_Wq, L0_attn_Wk, L0_attn_Wv, L0_attn_Wo, L0_attn_bo)
    x = x + _L0_ffn_ref(_layernorm(x, axis=-1), L0_ffn_gate_w, L0_ffn_gate_b, L0_ffn_bias, L0_ffn_w1, L0_ffn_b1, L0_ffn_w2, L0_ffn_b2)
    return x

_drawn_inputs = setup_inputs


def setup_inputs(seed=0):
    import zlib

    import numpy as np

    out = dict(_drawn_inputs(seed))
    spreads = {'L0_ffn_bias': (0.0, 0.1)}
    factors = {'L0_ffn_b1': 8.0, 'L0_ffn_b2': 8.0}
    for name, (base, spread) in spreads.items():
        noise = np.random.default_rng([zlib.crc32(name.encode()), seed]).standard_normal(out[name].shape)
        drawn = base * np.exp(spread * noise) if base else spread * noise
        out[name] = jnp.asarray(drawn.astype(out[name].dtype))
    for name, factor in factors.items():
        out[name] = (out[name] * factor).astype(out[name].dtype)
    return out
```

```python
from contextlib import ExitStack

import concourse.bass as bass
from concourse import mybir

F32 = mybir.dt.float32
F32R = mybir.dt.float32r
BF16 = mybir.dt.bfloat16
F16 = mybir.dt.float16
I32 = mybir.dt.int32
U32 = mybir.dt.uint32
ALU = mybir.AluOpType
ACT = mybir.ActivationFunctionType
AX_X = mybir.AxisListType.X
ds = bass.ds

P = 128
T = 2048
D = 512
INNER = 2048
HD = 64
NT = T // P
FB = D // P
CW = 512
NC = INNER // CW
CB = CW // P
HC = CW // HD
NP = INNER // P
E = 8
H = 352
EH = E * H
HB = 3
HR = H - 2 * P
W1T = EH // P
NS = T * 2 // P + E - 1
TW = NS + 1
EPS = 1e-5
KB = 1024
BASE = 16512


def block_kernel(nc, x, Wq, Wk, Wv, Wo, bo, gate_w, gate_b, gbias, w1, b1, w2, b2, out):
    xnT_dram = nc.dram_tensor("xnT_dram", (NT, P, D), F32, kind="Internal").ap()
    xn2_dram = nc.dram_tensor("xn2_dram", (T + P, D), F32, kind="Internal").ap()

    def sb(name, cols, at, dt=F32, parts=P):
        assert at + (2 if dt in (BF16, F16) else 4) * cols <= 229344 - BASE, name
        return nc.alloc_sbuf_tensor_at(name, [parts, cols], dt, offset=BASE + at)

    wk_hi = sb("wk_hi", FB * INNER, 0, F32R)
    wk_lo = sb("wk_lo", FB * INNER, 32 * KB, F32R)
    xn = sb("xn", NT * D, 64 * KB)
    xnT = sb("xnT", NT * D, 96 * KB)
    xnT_hi = sb("xnT_hi", 2 * D, 128 * KB, F32R)
    xnT_lo = sb("xnT_lo", 2 * D, 132 * KB, F32R)
    xn_hi = sb("xn_hi", 2 * D, 136 * KB, F32R)
    xn_lo = sb("xn_lo", 2 * D, 140 * KB, F32R)
    k_hi = sb("k_hi", 2 * CW, 144 * KB, F32R)
    k_lo = sb("k_lo", 2 * CW, 148 * KB, F32R)
    wk_in = sb("wk_in", FB * CW, 152 * KB)
    kacc = sb("kacc", INNER, 160 * KB)
    at = sb("at", FB * CW, 168 * KB)
    xn_new = sb("xn_new", 2 * D, 168 * KB)
    wv_in = sb("wv_in", 2 * D, 176 * KB)
    wo_in = sb("wo_in", 2 * D, 180 * KB)
    wv_hi = sb("wv_hi", D, 184 * KB, F32R)
    wv_lo = sb("wv_lo", D, 186 * KB, F32R)
    wo_hi = sb("wo_hi", D, 188 * KB, F32R)
    wo_lo = sb("wo_lo", D, 190 * KB, F32R)
    at_hl = sb("at_hl", 2 * D, 192 * KB, F32R)
    ks_hl = sb("ks_hl", 2 * P, 196 * KB, F32R)
    part = sb("part", 2 * P, 197 * KB)
    kvT = sb("kvT", P, 198 * KB)
    m_hi = sb("m_hi", 16 * D, 0, F32R)
    m_lo = sb("m_lo", 16 * D, 32 * KB, F32R)
    ksum = sb("ksum", INNER, 160 * KB)
    wq_in = sb("wq_in", FB * INNER, 128 * KB)
    wq_lo = sb("wq_lo", FB * INNER, 64 * KB, F32R)
    wq_hi = sb("wq_hi", FB * INNER, 96 * KB, F32R)
    xnT_in = sb("xnT_in", D, 168 * KB)
    qx_hi = sb("qx_hi", D, 170 * KB, F32R)
    qx_lo = sb("qx_lo", D, 172 * KB, F32R)
    q = sb("q", 2 * CW, 174 * KB)
    qk = sb("qk", CW, 178 * KB)
    qs = sb("qs", 2 * CW, 180 * KB)
    qsT_hi = sb("qsT_hi", 2 * CW, 184 * KB, F32R)
    qsT_lo = sb("qsT_lo", 2 * CW, 188 * KB, F32R)
    x_in = sb("x_in", D, 192 * KB)
    xb = sb("xb", D, 194 * KB)
    x2 = sb("x2", D, 128 * KB)
    xn2 = sb("xn2", D, 130 * KB)
    xn2T = sb("xn2T", D, 132 * KB)
    M0 = 200 * KB
    ident = sb("ident", P, M0)
    ones = sb("ones", P, M0 + 512, F32R)
    bd_hi = sb("bd_hi", P, M0 + 1024, F32R)
    bd_lo = sb("bd_lo", P, M0 + 2048, F32R)
    bo_b = sb("bo_b", D, M0 + 3072)
    scores = sb("scores", E, M0 + 5120)
    top8 = sb("top8", E, M0 + 5152)
    topi8 = sb("topi8", E, M0 + 5184, U32)
    gwT = sb("gwT", FB * E, M0 + 5632)
    gb_b = sb("gb_b", E, M0 + 5760)
    gb2_b = sb("gb2_b", E, M0 + 5792)
    gw_in = sb("gw_in", D, 166 * KB, parts=E)
    b1_in = sb("b1_in", H, 164 * KB, parts=E)
    b2_in = sb("b2_in", P, 162 * KB, parts=FB * E)
    eps = sb("eps", 1, M0 + 5824)
    st6 = sb("st6", 6, M0 + 5856)
    mv = sb("mv", 2, M0 + 5888)
    rs = sb("rs", 5, M0 + 5920)
    nrm = sb("nrm", 3 * HC, M0 + 5952)
    top = sb("top", NT * E, M0 + 6048)
    topi = sb("topi", NT * E, M0 + 6560, U32)
    slot_token = sb("slot_token", TW, M0 + 7072, I32)
    slot_gate = sb("slot_gate", TW, M0 + 7232)
    tile_expert = sb("tile_expert", TW, M0 + 7392, I32)
    b1T = sb("b1T", HB * E, M0 + 7552)
    gidx = sb("gidx", 2, M0 + 7648, I32)
    sidx = sb("sidx", 2, M0 + 7680, I32)
    b2T = sb("b2T", FB * E, M0 + 7712)
    zero = sb("zero", D, 198 * KB)
    w1_hi = sb("w1_hi", FB * EH, 0, F32R)
    w1_lo = sb("w1_lo", FB * EH, 44 * KB, F32R)
    w2_hi = sb("w2_hi", E * HB * D, 88 * KB, F32R)
    w2_lo = sb("w2_lo", E * HB * D, 136 * KB, F32R)
    w1_at = [134 * KB + k * 4 * D for k in range(11)] + [182400, 182400 + 4 * D] + [(104 + 2 * k) * KB for k in range(9)]
    w1_in = [sb(f"w1_in{k}", D, w1_at[k]) for k in range(W1T)]
    W2C = H + 1
    w2_at = [156 * KB, 156 * KB + 5664, 156 * KB + 2 * 5664, 156 * KB + 3 * 5664, 122 * KB, 122 * KB + 5664,
             184 * KB, 184 * KB + 5664]
    w2_in = [sb(f"w2_in{e}", FB * W2C, w2_at[e]) for e in range(E)]
    R0 = 88 * KB
    slot_val = sb("slot_val", 2 * NT * 3 * TW, R0, F32R)
    hot = sb("hot", 2 * NT * E, R0 + 15360)
    RH = 4
    row_hot = sb("row_hot", RH * P, M0 + 1024, F32R)
    slot_of = sb("slot_of", NT * E, M0 + 3072)
    prod = sb("prod", 2 * NT * E, M0 + 3584)
    mask = sb("mask", (NT + 1) * E, M0 + 4608, BF16)
    R1 = 182400 + 8 * D
    ch = sb("ch", 9 * 32, R1)
    ch_i = sb("ch_i", 3 * 32, R1 + 1152, I32)
    gate_hl = sb("gate_hl", 2 * 32, R1 + 1536, F32R)
    R2 = 196 * KB
    iota_e = sb("iota_e", E, R2)
    iota_j = sb("iota_j", TW, R2 + 32)
    k128 = sb("k128", NT, R2 + 192)
    tri8 = sb("tri8", E * E, R2 + 256)
    pad = sb("pad", 1, R2 + 512)
    iota_r = sb("iota_r", P, R2 + 544, F16)
    idp = sb("idp", 2 * NT, R2 + 800, F16)
    before = sb("before", P, R2 + 864, BF16)
    ones_b = sb("ones_b", P, R2 + 1120, BF16)
    cmp = sb("cmp", TW * E, R2 + 1536)
    small = sb("small", 4 * E, R2 + 2816)
    table = sb("table", 3 * TW, R2 + 2944)
    padt = sb("padt", TW, R2 + 3424)
    iota32 = sb("iota32", TW, R2 + 1536, I32)
    iota_r32 = sb("iota_r32", P, R2 + 2048, I32)
    gT_hi = sb("gT_hi", D, 184 * KB, F32R)
    gT_lo = sb("gT_lo", D, 186 * KB, F32R)
    h_in = sb("h_in", H, 188 * KB)
    hT = sb("hT", HB * P, 188 * KB + 1408)
    hT_hi = sb("hT_hi", HB * P, 190 * KB + 896, F32R)
    hT_lo = sb("hT_lo", HB * P, 192 * KB + 384, F32R)
    xg = sb("xg", 2 * D, 196 * KB)
    y = sb("y", 2 * D, M0 + 1024)

    with ExitStack() as ctx:
        def pb(name, n=1):
            return ctx.enter_context(nc.psum_tensor(name, [P, n * 512], F32))

        def sem(name):
            return ctx.enter_context(nc.semaphore(name))

        pA = pb("pA", 4)
        pK = pb("pK", 2)
        pT = pb("pT", 1)
        pX = pb("pX", 1)

        s_x = [sem(f"s_x{i}") for i in range(4)]
        s_gw = sem("s_gw")
        s_wk = sem("s_wk")
        s_small = sem("s_small")
        s_wv = [sem(f"s_wv{i}") for i in range(2)]
        s_wq = [sem(f"s_wq{i}") for i in range(NC)]
        xnT_stored = sem("xnT_stored")
        ident_ready = sem("ident_ready")
        pool_own = sem("pool_own")
        pool_link = sem("pool_link")
        consts_ready = sem("consts_ready")
        gwT_put = sem("gwT_put")
        gwT_ready = sem("gwT_ready")
        bn_stats_done = sem("bn_stats_done")
        rstd_step = sem("rstd_step")
        qk_ready = sem("qk_ready")
        nsum_ready = sem("nsum_ready")
        nclip_ready = sem("nclip_ready")
        nrec_ready = sem("nrec_ready")
        score_sum = sem("score_sum")
        var_ready = sem("var_ready")
        sqrt_ready = sem("sqrt_ready")
        xn_ready = sem("xn_ready")
        xn_kept = sem("xn_kept")
        xnT_put = sem("xnT_put")
        xnT_ready = sem("xnT_ready")
        xnT_hi_ready = sem("xnT_hi_ready")
        xnT_lo_ready = sem("xnT_lo_ready")
        xn_hi_ready = sem("xn_hi_ready")
        xn_lo_ready = sem("xn_lo_ready")
        wk_hi_ready = sem("wk_hi_ready")
        wk_lo_ready = sem("wk_lo_ready")
        kproj_done = sem("kproj_done")
        k_hi_ready = sem("k_hi_ready")
        k_lo_ready = sem("k_lo_ready")
        a_done = sem("a_done")
        kacc_done = sem("kacc_done")
        at_act = sem("at_act")
        at_dve = sem("at_dve")

        c_hi_ready = sem("c_hi_ready")
        c_lo_ready = sem("c_lo_ready")
        kv_put = sem("kv_put")
        part_ready = sem("part_ready")
        kv_ready = sem("kv_ready")
        kv_hi_ready = sem("kv_hi_ready")
        kv_lo_ready = sem("kv_lo_ready")
        m_put = sem("m_put")
        m_hi_ready = sem("m_hi_ready")
        m_lo_ready = sem("m_lo_ready")

        wq_hi_ready = sem("wq_hi_ready")
        wq_lo_ready = sem("wq_lo_ready")
        s_xnTin = sem("s_xnTin")
        qx_hi_ready = sem("qx_hi_ready")
        qx_lo_ready = sem("qx_lo_ready")
        q_put = sem("q_put")
        q_ready = sem("q_ready")
        qs_ready = sem("qs_ready")
        qsT_put = sem("qsT_put")
        qsT_hi_ready = sem("qsT_hi_ready")
        qsT_lo_ready = sem("qsT_lo_ready")
        o_put = sem("o_put")
        s_xin = sem("s_xin")
        xb_ready = sem("xb_ready")
        x2_ready = sem("x2_ready")
        x2_stored = sem("x2_stored")
        xn2_ready = sem("xn2_ready")
        xn2_stored = sem("xn2_stored")
        xn2T_put = sem("xn2T_put")
        xn2T_ready = sem("xn2T_ready")
        score_put = sem("score_put")
        score_ready = sem("score_ready")
        dump_stored = sem("dump_stored")
        zero_ready = sem("zero_ready")
        r_consts = sem("r_consts")
        top_done = sem("top_done")
        topi_done = sem("topi_done")
        top_kept = sem("top_kept")
        s_w1a = sem("s_w1a")
        s_w1b = sem("s_w1b")
        s_w2 = [sem(f"s_w2{e}") for e in range(E)]
        b2_put = sem("b2_put")
        w_put = sem("w_put")
        w_hi_ready = sem("w_hi_ready")
        w_lo_ready = sem("w_lo_ready")
        r_chain = sem("r_chain")
        gap_ready = sem("gap_ready")
        exp_ready = sem("exp_ready")
        mask_ready = sem("mask_ready")
        rank_put = sem("rank_put")
        vals_ready = sem("vals_ready")
        row_hot_ready = sem("row_hot_ready")
        row_hot_used = sem("row_hot_used")
        table_ready = sem("table_ready")
        slots_ready = sem("slots_ready")
        hT_ones = sem("hT_ones")
        s_g = [sem(f"s_g{i}") for i in range(2)]
        s_add = sem("s_add")
        gidx_ready = sem("gidx_ready")
        sidx_ready = sem("sidx_ready")
        gT_put = sem("gT_put")
        gT_hi_ready = sem("gT_hi_ready")
        gT_lo_ready = sem("gT_lo_ready")
        h_put = sem("h_put")
        h_ready = sem("h_ready")
        hT_put = sem("hT_put")
        hT_ready = sem("hT_ready")
        hT_hi_ready = sem("hT_hi_ready")
        hT_lo_ready = sem("hT_lo_ready")
        y_put = sem("y_put")
        y_ready = sem("y_ready")

        w1_rows = w1.rearrange("e h d -> (e h) d")
        WSTEPS = W1T + E * HB

        def w_step(k, w1_to, w2_to):
            bank = pA[:, (k % 4) * 512:(k % 4 + 1) * 512]
            if k < W1T:
                return bank.rearrange("p (f n) -> p f n", f=FB), P, \
                    w1_to[:, :].rearrange("p (f n) -> p f n", f=FB)[:, :, k * P:(k + 1) * P]
            w = min(P, W2C - (k - W1T) % HB * P)
            return bank[0:w], w, w2_to[0:w, (k - W1T) * D:(k - W1T + 1) * D]

        block = ctx.enter_context(nc.Block())
        f = lambda a: a.bitcast(F32)
        blocks = lambda a: a[:, :].rearrange("p (f n) -> p f n", f=FB)
        hl = lambda a: a[:, :].rearrange("p (f n) -> p f n", f=FB)
        halves = lambda a: a[:, :].rearrange("p (a n) -> p a n", a=2)

        @block.sync
        def _(sp):
            def load_wk(c):
                sp.dma_start(wk_in[:, :].rearrange("p (f n) -> p f n", f=FB),
                             Wk[:, c * CW:(c + 1) * CW].rearrange("(f p) n -> p f n", p=P)).then_inc(s_wk, 16)

            for g in range(4):
                for t in range(4 * g, 4 * g + 4):
                    sp.dma_start(xn[:, t * D:(t + 1) * D], x[t * P:(t + 1) * P, :]).then_inc(s_x[g], 16)
                if g == 0:
                    load_wk(0)
                    sp.dma_start(gw_in[:, :], gate_w).then_inc(s_gw, 16)
                    sp.dma_start(b1_in[:, :], b1).then_inc(s_gw, 16)
                    sp.dma_start(b2_in[:, :], b2.rearrange("e (f n) -> (e f) n", n=P)).then_inc(s_gw, 16)
            sp.dma_start(bo_b[:, :], bo.partition_broadcast(P)).then_inc(s_small, 16)
            sp.dma_start(gb_b[:, :], gate_b.partition_broadcast(P)).then_inc(s_small, 16)
            sp.dma_start(gb2_b[:, :], gbias.partition_broadcast(P)).then_inc(s_small, 16)
            for c in range(1, NC):
                sp.wait_ge(wk_hi_ready, c)
                sp.wait_ge(wk_lo_ready, c)
                load_wk(c)
            sp.wait_ge(xnT_ready, NT)
            for g in range(4):
                sp.dma_start(xnT_dram[4 * g:4 * g + 4].rearrange("t p n -> p t n"),
                             xnT[:, 4 * g * D:4 * (g + 1) * D].rearrange("p (t n) -> p t n", t=4)
                             ).then_inc(xnT_stored, 16)

            def load_pair(n, b):
                sp.dma_start(wv_in[:, b * D:(b + 1) * D].rearrange("p (f n) -> p f n", f=FB),
                             Wv[:, ds(n * P, P)].rearrange("(f p) n -> p f n", p=P)).then_inc(s_wv[b], 16)
                sp.dma_start(wo_in[:, b * D:(b + 1) * D], Wo[ds(n * P, P), :]).then_inc(s_wv[b], 16)

            load_pair(0, 0)
            load_pair(1, 1)
            with sp.Fori(1, NP // 2) as h:
                for b in range(2):
                    sp.wait_ge(c_lo_ready, 2 * h + (b - 1))
                    load_pair(2 * h + b, b)

            sp.wait_ge(xnT_hi_ready, NC * NT + 2)
            sp.wait_ge(xnT_lo_ready, NC * NT + 2)
            sp.wait_ge(xn_lo_ready, NC * NT + 1)
            sp.wait_ge(a_done, NC * NT)
            sp.wait_ge(kacc_done, NC * NT)
            for c in range(NC):
                sp.dma_start(wq_in[:, c * FB * CW:(c + 1) * FB * CW].rearrange("p (f n) -> p f n", f=FB),
                             Wq[:, c * CW:(c + 1) * CW].rearrange("(f p) n -> p f n", p=P)).then_inc(s_wq[c], 16)

            sp.wait_ge(m_put, NP)
            sp.wait_ge(m_lo_ready, NP)
            sp.dma_start(xnT_in[:, :], xnT_dram[0]).then_inc(s_xnTin, 16)
            sp.dma_start(x_in[:, :], x[0:P, :]).then_inc(s_xin, 16)
            sp.wait_ge(zero_ready, 1)
            sp.dma_start(out[T:T + P, :], zero[:, :]).then_inc(dump_stored, 16)
            sp.dma_start(xn2_dram[T:T + P, :], zero[:, :]).then_inc(dump_stored, 16)
            sp.wait_ge(qx_hi_ready, 1)
            sp.wait_ge(qx_lo_ready, 1)
            sp.dma_start(xnT_in[:, :], xnT_dram[1]).then_inc(s_xnTin, 16)
            sp.wait_ge(xb_ready, 1)
            sp.dma_start(x_in[:, :], x[P:2 * P, :]).then_inc(s_xin, 16)
            sp.wait_ge(wq_lo_ready, NC)
            for k in range(11):
                sp.dma_start(w1_in[k][:, :], w1_rows[k * P:(k + 1) * P, :]).then_inc(s_w1a, 16)
            with sp.Fori(1, NT - 1) as t:
                sp.wait_ge(qx_hi_ready, t + 1)
                sp.wait_ge(qx_lo_ready, t + 1)
                sp.dma_start(xnT_in[:, :], xnT_dram[ds(t + 1, 1)].rearrange("a p n -> (a p) n")).then_inc(s_xnTin, 16)
                sp.wait_ge(x2_ready, t)
                sp.dma_start(out[ds((t - 1) * P, P), :], x2[:, :]).then_inc(x2_stored, 16)
                sp.wait_ge(xb_ready, t + 1)
                sp.dma_start(x_in[:, :], x[ds((t + 1) * P, P), :]).then_inc(s_xin, 16)
                sp.wait_ge(xn2_ready, t)
                sp.dma_start(xn2_dram[ds((t - 1) * P, P), :], xn2[:, :]).then_inc(xn2_stored, 16)
            sp.wait_ge(x2_ready, NT - 1)
            sp.dma_start(out[(NT - 2) * P:(NT - 1) * P, :], x2[:, :]).then_inc(x2_stored, 16)
            sp.wait_ge(xn2_ready, NT - 1)
            sp.dma_start(xn2_dram[(NT - 2) * P:(NT - 1) * P, :], xn2[:, :]).then_inc(xn2_stored, 16)
            sp.wait_ge(q_put, NC * NT)
            for k in range(13, W1T):
                sp.dma_start(w1_in[k][:, :], w1_rows[k * P:(k + 1) * P, :]).then_inc(s_w1b, 16)
            sp.wait_ge(x2_ready, NT)
            sp.dma_start(out[(NT - 1) * P:NT * P, :], x2[:, :]).then_inc(x2_stored, 16)
            sp.wait_ge(xn2_ready, NT)
            sp.dma_start(xn2_dram[(NT - 1) * P:NT * P, :], xn2[:, :]).then_inc(xn2_stored, 16)

            def load_w2(e):
                sp.dma_start(w2_in[e][:, :].rearrange("p (f n) -> p f n", f=FB)[:, :, 0:H],
                             w2[e].rearrange("(f p) n -> p f n", p=P)).then_inc(s_w2[e], 16)

            for k in (11, 12):
                sp.dma_start(w1_in[k][:, :], w1_rows[k * P:(k + 1) * P, :]).then_inc(s_w1b, 16)
            for e in (0, 1, 2, 3, 4, 6, 7):
                load_w2(e)
            sp.wait_ge(x2_stored, 16 * NT)
            sp.wait_ge(xn2_stored, 16 * NT)
            sp.wait_ge(score_put, NT)
            load_w2(5)
            sp.wait_ge(s_add, 16 * NS)
            sp.wait_ge(x2_stored, 16 * NT)
            sp.wait_ge(dump_stored, 32)

        @block.gpsimd
        def _(pool):
            pool.memset(ident[:, :], 1.0).then_inc(pool_own, 1)
            pool.wait_ge(pool_own, 1)
            pool.affine_select(ident[:, :], ident[:, :], pattern=[[-1, P]], base=0, channel_multiplier=1,
                               compare_op=ALU.is_equal, fill=0.0).then_inc(ident_ready, 1)
            pool.memset(eps[:, :], EPS).then_inc(consts_ready, 1)
            pool.memset(f(ones[:, :]), 1.0).then_inc(consts_ready, 1)
            pool.memset(f(bd_hi[:, :]), 0.0).then_inc(consts_ready, 1)
            pool.memset(f(bd_lo[:, :]), 0.0).then_inc(consts_ready, 1)
            pool.wait_ge(gwT_ready, 1)
            pool.memset(kacc[:, :], 0.0).then_inc(consts_ready, 1)
            pool.wait_ge(consts_ready, 5)

            linked = [0]

            def link(ins):
                linked[0] += 1
                ins.then_inc(pool_link, 1)
                pool.wait_ge(pool_link, linked[0])

            def add_k(c, n, b):
                acc = kacc[:, ds(c * CW, CW)]
                pool.wait_ge(k_hi_ready, n + 1)
                if not (isinstance(n, int) and n == 0):
                    pool.wait_ge(kacc_done, n)
                pool.nop(nofuse=True)
                pool.tensor_tensor(acc, acc, f(k_hi[:, b * CW:(b + 1) * CW]), ALU.add).then_inc(pool_own, 1)
                pool.wait_ge(pool_own, n + 2)
                pool.wait_ge(k_lo_ready, n + 1)
                pool.nop(nofuse=True)
                pool.tensor_tensor(acc, acc, f(k_lo[:, b * CW:(b + 1) * CW]), ALU.add).then_inc(kacc_done, 1)

            def keep_xn(t, b):
                pool.wait_ge(xn_ready, t + 1)
                pool.tensor_copy(xn[:, ds(t * D, D)], xn_new[:, b * D:(b + 1) * D]).then_inc(xn_kept, 1)

            for t in range(4):
                keep_xn(t, t % 2)
            for b in range(2):
                keep_xn(4 + b, b)
                add_k(0, b, b)
            with pool.Fori(1, NT // 2 - 2) as p:
                for b in range(2):
                    keep_xn(2 * p + (4 + b), b)
                    add_k(0, 2 * p + b, b)
            with pool.Fori(NT // 2 - 2, NT // 2) as p:
                for b in range(2):
                    add_k(0, 2 * p + b, b)
            with pool.Fori(1, NC) as c:
                with pool.Fori(0, NT // 2) as p:
                    for b in range(2):
                        add_k(c, c * NT + 2 * p + b, b)

            pool.wait_ge(m_lo_ready, NP)
            pool.wait_ge(m_put, NP)
            pool.memset(zero[:, :], 0.0).then_inc(zero_ready, 1)
            link(pool.iota(iota32[:, 0:E], pattern=[[1, E]], base=0, channel_multiplier=0))
            link(pool.tensor_copy(iota_e[:, :], iota32[:, 0:E]))
            link(pool.iota(iota32[:, 0:TW], pattern=[[1, TW]], base=0, channel_multiplier=0))
            link(pool.tensor_copy(iota_j[:, :], iota32[:, 0:TW]))
            link(pool.iota(iota32[:, 0:NT], pattern=[[P, NT]], base=0, channel_multiplier=0))
            link(pool.tensor_copy(k128[:, :], iota32[:, 0:NT]))
            link(pool.iota(iota32[:, 0:1], pattern=[[1, 1]], base=T + 1, channel_multiplier=1))
            link(pool.tensor_copy(pad[:, :], iota32[:, 0:1]))
            link(pool.iota(iota32[:, 0:2 * NT], pattern=[[0, 2], [P, NT]], base=1, channel_multiplier=1))
            link(pool.tensor_copy(idp[:, :], iota32[:, 0:2 * NT]))
            link(pool.memset(tri8[:, :], 1.0))
            link(pool.affine_select(tri8[:, :].rearrange("p (a b) -> p a b", a=E), tri8[:, :].rearrange("p (a b) -> p a b", a=E),
                                    pattern=[[1, E], [-1, E]], base=0, channel_multiplier=0,
                                    compare_op=ALU.is_ge, fill=0.0))
            link(pool.memset(ones_b[:, :], 1.0))
            link(pool.affine_select(before[:, :], ones_b[:, :], pattern=[[1, P]], base=0, channel_multiplier=-1,
                                    compare_op=ALU.is_gt, fill=0.0))
            pool.wait_ge(dump_stored, 32)
            link(pool.iota(iota_r32[:, :], pattern=[[1, P]], base=0, channel_multiplier=0))
            pool.tensor_copy(iota_r[:, :], iota_r32[:, :]).then_inc(r_consts, 1)

            pool.wait_ge(s_small, 16 * 3)
            pool.wait_ge(s_xin, 16)
            pool.tensor_tensor(xb[:, :], x_in[:, :], bo_b[:, :], ALU.add).then_inc(xb_ready, 1)
            with pool.Fori(1, NT) as t:
                pool.wait_ge(s_xin, 16 * t + 16)
                pool.wait_ge(x2_ready, t)
                pool.tensor_tensor(xb[:, :], x_in[:, :], bo_b[:, :], ALU.add).then_inc(xb_ready, 1)

            pool.wait_ge(x2_ready, NT)
            pool.wait_ge(qs_ready, NC * NT)
            pool.wait_ge(o_put, NC * NT)
            pool.wait_ge(x2_stored, 16 * NT)
            pool.wait_ge(xn2_stored, 16 * NT)
            pool.wait_ge(score_put, NT)
            for e in range(E):
                pool.tensor_copy(w2_in[e][:, :].rearrange("p (f n) -> p f n", f=FB)[:, :, H:H + 1],
                                 b2T[:, e * FB:(e + 1) * FB].unsqueeze(2)).then_inc(b2_put, 1)

            pool.wait_ge(slots_ready, 1)
            pool.wait_ge(dump_stored, 32)

            def gather(i, b, first=False):
                if not first:
                    pool.wait_ge(gT_put, i - 1)
                pool.tensor_copy(gidx[:, b:b + 1], slot_token[:, ds(i, 1)]).then_inc(gidx_ready, 1)
                pool.wait_ge(gidx_ready, i + 1)
                pool.nop(nofuse=True)
                pool.indirect_dma_start(xg[:, b * D:(b + 1) * D], None, xn2_dram,
                                        bass.IndirectOffsetOnAxis(gidx[:, b:b + 1].bitcast(U32), 0)).then_inc(s_g[b], 16)

            def add_out(i, b, first=False):
                if not first:
                    pool.wait_ge(s_add, 16 * i)
                pool.wait_ge(y_ready, i + 1)
                pool.tensor_copy(sidx[:, b:b + 1], slot_token[:, ds(i, 1)]).then_inc(sidx_ready, 1)
                pool.wait_ge(sidx_ready, i + 1)
                pool.nop(nofuse=True)
                pool.indirect_dma_start(out, bass.IndirectOffsetOnAxis(sidx[:, b:b + 1].bitcast(U32), 0),
                                        y[:, b * D:(b + 1) * D], None, compute_op=ALU.add).then_inc(s_add, 16)

            gather(0, 0, True)
            gather(1, 1, True)
            gather(2, 0)
            gather(3, 1)
            add_out(0, 0, True)
            with pool.Fori(1, NS // 2 - 1) as h:
                for b in range(2):
                    gather(2 * h + (b + 2), b)
                    add_out(2 * h + (b - 1), 1 - b)
            gather(NS - 1, 0)
            for i in range(NS - 4, NS):
                add_out(i, i % 2)

        @block.scalar
        def _(act):
            def split_wk(c):
                act.wait_ge(s_wk, 16 * c + 16)
                for b in range(FB):
                    i = nc.scalar.copy(wk_hi[:, (c * FB + b) * CW:(c * FB + b + 1) * CW],
                                       wk_in[:, b * CW:(b + 1) * CW])
                i.then_inc(wk_hi_ready, 1)

            def sqrt_var(t):
                act.wait_ge(var_ready, t + 1)
                nc.scalar.activation(rs[:, 0:1], mv[:, 1:2], ACT.Sqrt, bias=eps[:, :]).then_inc(sqrt_ready, 1)

            def put_xnT(t):
                act.wait_ge(xnT_put, t + 1)
                nc.scalar.copy(xnT[:, ds(t * D, D)], pT[:, :]).then_inc(xnT_ready, 1)

            def split_xnT(n, t, b):
                if isinstance(n, int) and n < 2:
                    act.wait_ge(xnT_ready, n + 1)
                else:
                    act.wait_ge(kproj_done, n - 1)
                    act.nop(nofuse=True)
                nc.scalar.copy(xnT_hi[:, b * D:(b + 1) * D], xnT[:, ds(t * D, D)]).then_inc(xnT_hi_ready, 1)

            def split_xn(n, t, b):
                if not (isinstance(n, int) and n < 2):
                    act.wait_ge(a_done, n - 1)
                nc.scalar.copy(xn_hi[:, b * D:(b + 1) * D], xn[:, ds(t * D, D)]).then_inc(xn_hi_ready, 1)

            def split_k(n, b):
                act.wait_ge(kproj_done, n + 1)
                if not (isinstance(n, int) and n < 2):
                    act.wait_ge(a_done, n - 1)
                    act.wait_ge(kacc_done, n - 1)
                nc.scalar.activation(k_hi[:, b * CW:(b + 1) * CW], pK[:, b * 512:(b + 1) * 512],
                                     ACT.Relu).then_inc(k_hi_ready, 1)

            def put_at(c):
                act.wait_ge(a_done, c * NT + NT)
                for b in range(2):
                    i = nc.scalar.copy(at[:, b * CW:(b + 1) * CW], pA[:, b * 512:(b + 1) * 512])
                i.then_inc(at_act, 1)

            act.wait_ge(consts_ready, 1)
            act.wait_ge(gwT_put, 1)
            nc.scalar.copy(gwT[:, :], pX[:, 0:FB * E])
            nc.scalar.copy(b1T[:, 0:2 * E], pX[:, 32:32 + 2 * E])
            nc.scalar.copy(b1T[0:HR, 2 * E:3 * E], pX[0:HR, 32 + 2 * E:32 + 3 * E])
            nc.scalar.copy(b2T[:, :], pX[:, 64:96]).then_inc(gwT_ready, 1)
            sqrt_var(0)
            split_wk(0)
            for t in range(1, 4):
                sqrt_var(t)
                if t >= 2:
                    put_xnT(t - 2)
                    split_xnT(t - 2, t - 2, t - 2)
            act.wait_ge(xn_kept, 1)
            split_xn(0, 0, 0)

            def chunk0_pair(p):
                for b in range(2):
                    n = 2 * p + b
                    if not isinstance(p, int) or p < 6:
                        sqrt_var(n + 4)
                    if not isinstance(p, int) or p < 7:
                        put_xnT(n + 2)
                    split_k(n, b)
                    if not isinstance(p, int) or p < 7:
                        act.wait_ge(xnT_ready, n + 3)
                        split_xnT(n + 2, n + 2, b)
                        act.wait_ge(xn_kept, n + 2)
                    else:
                        split_xnT(n + 2, b, b)
                    split_xn(n + 1, (n + 1) % NT if isinstance(p, int) else n + 1, 1 - b)

            chunk0_pair(0)
            split_wk(1)
            with act.Fori(1, 6) as p:
                chunk0_pair(p)
            chunk0_pair(6)
            split_wk(2)
            chunk0_pair(7)
            split_wk(3)
            put_at(0)

            def act_pair(n, j, b, jn=None):
                act.wait_ge(s_wv[b], jn)
                nc.scalar.copy(wv_hi[:, :], wv_in[:, b * D:(b + 1) * D])
                nc.scalar.copy(wo_hi[:, :], wo_in[:, b * D:(b + 1) * D])
                nc.scalar.copy(hl(at_hl)[:, :, 0:P], blocks(at)[:, :, j * P:(j + 1) * P])
                nc.scalar.copy(ks_hl[:, 0:P], kacc[:, ds(n * P, P)]).then_inc(c_hi_ready, 1)

            def act_kv(n):
                act.wait_ge(kv_put, n + 1)
                nc.scalar.copy(part[:, :].rearrange("p (a n) -> p a n", a=2), halves(pT)[:, :, P:2 * P]).then_inc(part_ready, 1)
                act.wait_ge(kv_ready, n + 1)
                for h in range(2):
                    s = slice(h * HD, (h + 1) * HD)
                    i = nc.scalar.copy(bd_hi[s, s], kvT[s, s])
                i.then_inc(kv_hi_ready, 1)

            def act_m(n):
                act.wait_ge(m_put, n + 1)
                nc.scalar.copy(m_hi[:, ds(n * D, D)], pX[:, :]).then_inc(m_hi_ready, 1)

            def at_ready(c):
                act.wait_ge(kacc_done, c * NT)
                act.wait_ge(at_act, c)
                act.wait_ge(at_dve, c)

            def act_steps(c, j, last):
                for i in range(4):
                    n = c * NT + 4 * j + i
                    split_k(n, i % 2)
                    split_xnT(n + 2, (i - 2 if last and i >= 2 else 4 * j + (i + 2)), i % 2)
                    split_xn(n + 1, (0 if last and i == 3 else 4 * j + (i + 1)), 1 - i % 2)
                    pair = 4 * (c - 1) + j
                    if i == 0:
                        act_pair(pair, j, j % 2, 32 * (2 * (c - 1) + j // 2) + 32)
                    if i == 2:
                        act_kv(pair)
                    if i == 3:
                        act_m(pair)

            with act.Fori(1, NC) as c:
                at_ready(c)
                for j in range(4):
                    act_steps(c, j, j == 3)
                put_at(c)
            at_ready(NC)
            for j in range(4):
                act_pair(NP - 4 + j, j, j % 2, 32 * (NP // 2 - 2 + j // 2) + 32)
                act_kv(NP - 4 + j)
                act_m(NP - 4 + j)

            act.wait_ge(xnT_lo_ready, NC * NT + 2)
            act.wait_ge(xn_lo_ready, NC * NT + 1)
            act.wait_ge(xnT_stored, 64)
            for c in range(NC):
                act.wait_ge(s_wq[c], 16)
                nc.scalar.copy(wq_hi[:, c * 2048:(c + 1) * 2048], wq_in[:, c * 2048:(c + 1) * 2048]).then_inc(wq_hi_ready, 1)
                if c == 0:
                    act.wait_ge(s_xnTin, 16)
                    nc.scalar.copy(qx_hi[:, :], xnT_in[:, :]).then_inc(qx_hi_ready, 1)

            def act_q(m, c, first):
                act.wait_ge(q_put, m + 1)
                if not (first and c < 2):
                    act.wait_ge(qs_ready, m - 1)
                nc.scalar.activation(q[:, (c % 2) * CW:(c % 2 + 1) * CW], pK[:, (c % 2) * 512:(c % 2 + 1) * 512],
                                     ACT.Relu).then_inc(q_ready, 1)

            def act_qsT(m, b):
                act.wait_ge(qsT_put, m + 1)
                if not (isinstance(m, int) and m < 2):
                    act.wait_ge(o_put, m - 1)
                nc.scalar.copy(qsT_hi[:, b * CW:(b + 1) * CW], pA[:, (2 + b) * 512:(3 + b) * 512]).then_inc(qsT_hi_ready, 1)

            def act_qx(t):
                act.wait_ge(q_put, 4 * t)
                act.wait_ge(s_xnTin, 16 * t + 16)
                nc.scalar.copy(qx_hi[:, :], xnT_in[:, :]).then_inc(qx_hi_ready, 1)

            def act_xn2T(t):
                act.wait_ge(xn2T_put, t + 1)
                nc.scalar.copy(xn2T[:, :], pT[:, :]).then_inc(xn2T_ready, 1)

            for c in range(NC):
                act_q(c, c, True)
                if c >= 1:
                    act_qsT(c - 1, (c - 1) % 2)
            act_qx(1)

            def act_tile(t, last):
                for c in range(NC):
                    m = 4 * t + c
                    act_q(m, c, False)
                    if c == 3 and not last:
                        act_qx(t + 1)
                    if c == 3:
                        act_xn2T(t - 1)
                    act_qsT(m - 1, (c - 1) % 2)
                    if c == 2:
                        sqrt_var(NT + t - 1)

            with act.Fori(1, NT - 1) as t:
                act_tile(t, False)
            act_tile(NT - 1, True)
            act_qsT(4 * NT - 1, 1)
            sqrt_var(2 * NT - 1)
            act_xn2T(NT - 1)

            act.wait_ge(gap_ready, 1)
            nc.scalar.activation(ch[:, 16:32], ch[:, 0:16], ACT.Exp).then_inc(exp_ready, 1)

            def w_hi(k):
                act.wait_ge(w_put, k + 1)
                src, rows, dst = w_step(k, w1_hi, w2_hi)
                nc.scalar.copy(dst, src).then_inc(w_hi_ready, 1)

            for k in range(7):
                w_hi(k)
            act.wait_ge(row_hot_used, 32)
            nc.scalar.copy(table[:, :], pX[:, 0:3 * TW]).then_inc(table_ready, 1)
            for k in range(7, WSTEPS):
                w_hi(k)

            def act_gT(i):
                act.wait_ge(gT_put, i + 1)
                if not (isinstance(i, int) and i == 0):
                    act.wait_ge(h_put, i)
                nc.scalar.copy(gT_hi[:, :], pT[:, :]).then_inc(gT_hi_ready, 1)

            def act_h(i):
                act.wait_ge(h_put, i + 1)
                if not (isinstance(i, int) and i == 0):
                    act.wait_ge(hT_put, i)
                nc.scalar.copy(h_in[:, :], pK[:, 0:H]).then_inc(h_ready, 1)

            def act_silu(i, e):
                act.wait_ge(hT_put, i + 1)
                if not (isinstance(i, int) and i == 0):
                    act.wait_ge(hT_lo_ready, i)
                for b in range(HB):
                    w = min(P, H - b * P)
                    last = nc.scalar.activation(hT[0:w, b * P:(b + 1) * P], pX[0:w, b * P:(b + 1) * P], ACT.Silu,
                                                bias=b1T[0:w, ds(b * E + e, 1)])
                last.then_inc(hT_ready, 1)

            def act_tile_e(i, last=False):
                act_h(i)
                if not last:
                    act_gT(i + 1)
                e = act.value_load(tile_expert[0:1, ds(i, 1)], min_val=0, max_val=E - 1)
                act_silu(i, e)

            act.wait_ge(slots_ready, 1)
            act.wait_ge(hT_ones, 1)
            act.wait_ge(w_put, WSTEPS)
            act_gT(0)
            act_tile_e(0)
            with act.Fori(1, NS - 1) as i:
                act_tile_e(i)
            act_tile_e(NS - 1, True)

        @block.vector
        def _(dve):
            def newton_rstd(n):
                dve.wait_ge(sqrt_ready, n + 1)
                nc.vector.reciprocal(rs[:, 1:2], rs[:, 0:1]).then_inc(rstd_step, 1)
                dve.wait_ge(rstd_step, 4 * n + 1)
                nc.vector.tensor_scalar(rs[:, 2:3], mv[:, 1:2], EPS, rs[:, 1:2], ALU.add, ALU.mult).then_inc(rstd_step, 1)
                dve.wait_ge(rstd_step, 4 * n + 2)
                nc.vector.tensor_scalar(rs[:, 3:4], rs[:, 2:3], rs[:, 1:2], -0.5, ALU.mult, ALU.mult).then_inc(rstd_step, 1)
                dve.wait_ge(rstd_step, 4 * n + 3)
                nc.vector.tensor_scalar(rs[:, 4:5], rs[:, 3:4], 1.5, rs[:, 1:2], ALU.add, ALU.mult).then_inc(rstd_step, 1)
                dve.wait_ge(rstd_step, 4 * n + 4)

            def stats(src, n):
                nc.vector.bn_stats(st6[:, :], src).then_inc(bn_stats_done, 1)
                dve.wait_ge(bn_stats_done, n + 1)
                dve.nop(nofuse=True)
                nc.vector.bn_aggr(mv[:, :], st6[:, :]).then_inc(var_ready, 1)

            def normalize(dst, src):
                return nc.vector.tensor_scalar(dst, src, mv[:, 0:1], rs[:, 4:5], ALU.subtract, ALU.mult)

            def layernorm1(t, b):
                stats(xn[:, ds(t * D, D)], t)
                newton_rstd(t)
                if not (isinstance(t, int) and t < 2):
                    dve.wait_ge(xnT_put, t - 1)
                    dve.wait_ge(xn_kept, t - 1)
                normalize(xn_new[:, b * D:(b + 1) * D], xn[:, ds(t * D, D)]).then_inc(xn_ready, 1)

            def lo(dst, src, hi):
                return nc.vector.tensor_tensor(dst, src, f(hi), ALU.subtract)

            def split_wk(c):
                dve.wait_ge(wk_hi_ready, c + 1)
                for b in range(FB):
                    s = slice((c * FB + b) * CW, (c * FB + b + 1) * CW)
                    i = lo(wk_lo[:, s], wk_in[:, b * CW:(b + 1) * CW], wk_hi[:, s])
                i.then_inc(wk_lo_ready, 1)

            def split_xnT(n, t, b):
                dve.wait_ge(xnT_hi_ready, n + 1)
                s = slice(b * D, (b + 1) * D)
                lo(xnT_lo[:, s], xnT[:, ds(t * D, D)], xnT_hi[:, s]).then_inc(xnT_lo_ready, 1)

            def split_xn(n, t, b):
                dve.wait_ge(xn_hi_ready, n + 1)
                s = slice(b * D, (b + 1) * D)
                lo(xn_lo[:, s], xn[:, ds(t * D, D)], xn_hi[:, s]).then_inc(xn_lo_ready, 1)

            def split_k(n, b):
                dve.wait_ge(k_hi_ready, n + 1)
                s = slice(b * CW, (b + 1) * CW)
                nc.vector.scalar_tensor_tensor(out=k_lo[:, s], in0=pK[:, b * 512:(b + 1) * 512], scalar=0.0,
                                               in1=f(k_hi[:, s]), op0=ALU.max, op1=ALU.subtract
                                               ).then_inc(k_lo_ready, 1)

            def put_at(c):
                dve.wait_ge(a_done, c * NT + NT)
                for b in range(2, 4):
                    i = nc.vector.tensor_copy(at[:, b * CW:(b + 1) * CW], pA[:, b * 512:(b + 1) * 512])
                i.then_inc(at_dve, 1)

            dve.wait_ge(s_x[0], 64)
            layernorm1(0, 0)
            split_wk(0)
            for t in range(1, 4):
                layernorm1(t, t % 2)
                if t >= 2:
                    split_xnT(t - 2, t - 2, t - 2)
            split_xn(0, 0, 0)

            def chunk0_pair(p):
                for b in range(2):
                    n = 2 * p + b
                    if not isinstance(p, int) or p < 6:
                        layernorm1(n + 4, b)
                    split_k(n, b)
                    split_xnT(n + 2, n + 2 if not isinstance(p, int) else (n + 2) % NT, b)
                    split_xn(n + 1, n + 1 if not isinstance(p, int) else (n + 1) % NT, 1 - b)

            dve.wait_ge(s_x[1], 64)
            chunk0_pair(0)
            split_wk(1)
            dve.wait_ge(s_x[2], 64)
            dve.wait_ge(s_x[3], 64)
            with dve.Fori(1, 6) as p:
                chunk0_pair(p)
            chunk0_pair(6)
            split_wk(2)
            chunk0_pair(7)
            split_wk(3)
            put_at(0)

            def dve_pair(n, j, b):
                dve.wait_ge(c_hi_ready, n + 1)
                lo(wv_lo[:, :], wv_in[:, b * D:(b + 1) * D], wv_hi[:, :])
                lo(wo_lo[:, :], wo_in[:, b * D:(b + 1) * D], wo_hi[:, :])
                nc.vector.tensor_tensor(hl(at_hl)[:, :, P:2 * P], blocks(at)[:, :, j * P:(j + 1) * P],
                                        f(hl(at_hl)[:, :, 0:P]), ALU.subtract)
                lo(ks_hl[:, P:2 * P], kacc[:, ds(n * P, P)], ks_hl[:, 0:P]).then_inc(c_lo_ready, 1)

            def dve_kv(n):
                dve.wait_ge(part_ready, n + 1)
                nc.vector.tensor_tensor(ksum[:, ds(n * P, P)], pT[:, 256:256 + P], part[:, P:2 * P], ALU.add)
                nc.vector.tensor_tensor(kvT[:, :], pT[:, 0:P], part[:, 0:P], ALU.add).then_inc(kv_ready, 1)
                dve.wait_ge(kv_hi_ready, n + 1)
                for h in range(2):
                    s = slice(h * HD, (h + 1) * HD)
                    i = lo(bd_lo[s, s], kvT[s, s], bd_hi[s, s])
                i.then_inc(kv_lo_ready, 1)

            def dve_m(n):
                dve.wait_ge(m_hi_ready, n + 1)
                lo(m_lo[:, ds(n * D, D)], pX[:, :], m_hi[:, ds(n * D, D)]).then_inc(m_lo_ready, 1)

            with dve.Fori(1, NC) as c:
                for j in range(4):
                    for i in range(4):
                        n = c * NT + (4 * j + i)
                        split_k(n, i % 2)
                        split_xnT(n + 2, (4 * j + i + 2) % NT, i % 2)
                        split_xn(n + 1, (4 * j + i + 1) % NT, 1 - i % 2)
                        pair = 4 * c + (j - 4)
                        if i == 0:
                            dve_pair(pair, j, j % 2)
                        if i == 2:
                            dve_kv(pair)
                        if i == 3:
                            dve_m(pair)
                put_at(c)
            for j in range(4):
                dve_pair(NP - 4 + j, j, j % 2)
                dve_kv(NP - 4 + j)
                dve_m(NP - 4 + j)

            for c in range(NC):
                dve.wait_ge(wq_hi_ready, c + 1)
                s = slice(c * 2048, (c + 1) * 2048)
                lo(wq_lo[:, s], wq_in[:, s], wq_hi[:, s]).then_inc(wq_lo_ready, 1)
                if c == 0:
                    dve.wait_ge(qx_hi_ready, 1)
                    lo(qx_lo[:, :], xnT_in[:, :], qx_hi[:, :]).then_inc(qx_lo_ready, 1)
            heads = lambda a: a.rearrange("p (h d) -> p h d", h=HC)

            def dve_q(m, c):
                b = c % 2
                dve.wait_ge(q_ready, m + 1)
                nc.vector.tensor_tensor(qk[:, :], q[:, b * CW:(b + 1) * CW], ksum[:, c * CW:(c + 1) * CW],
                                        ALU.mult).then_inc(qk_ready, 1)
                dve.wait_ge(qk_ready, m + 1)
                nc.vector.tensor_reduce(nrm[:, 0:HC], heads(qk[:, :]), AX_X, ALU.add).then_inc(nsum_ready, 1)
                dve.wait_ge(nsum_ready, m + 1)
                nc.vector.tensor_scalar(nrm[:, HC:2 * HC], nrm[:, 0:HC], 1e-6, None, ALU.max).then_inc(nclip_ready, 1)
                dve.wait_ge(nclip_ready, m + 1)
                nc.vector.reciprocal(nrm[:, 2 * HC:3 * HC], nrm[:, HC:2 * HC]).then_inc(nrec_ready, 1)
                dve.wait_ge(nrec_ready, m + 1)
                if not (isinstance(m, int) and m < 2):
                    dve.wait_ge(qsT_put, m - 1)
                nc.vector.tensor_tensor(heads(qs[:, b * CW:(b + 1) * CW]), heads(q[:, b * CW:(b + 1) * CW]),
                                        nrm[:, 2 * HC:3 * HC].unsqueeze(2).to_broadcast([P, HC, HD]),
                                        ALU.mult).then_inc(qs_ready, 1)

            def dve_qsT(m, b):
                dve.wait_ge(qsT_hi_ready, m + 1)
                s = slice(b * CW, (b + 1) * CW)
                lo(qsT_lo[:, s], pA[:, (2 + b) * 512:(3 + b) * 512], qsT_hi[:, s]).then_inc(qsT_lo_ready, 1)

            def dve_qx(t):
                dve.wait_ge(qx_hi_ready, t + 1)
                lo(qx_lo[:, :], xnT_in[:, :], qx_hi[:, :]).then_inc(qx_lo_ready, 1)

            def residual(t):
                dve.wait_ge(o_put, 4 * t + 4)
                dve.wait_ge(xb_ready, t + 1)
                if not (isinstance(t, int) and t == 0):
                    dve.wait_ge(x2_stored, 16 * t)
                nc.vector.tensor_tensor(x2[:, :], pX[:, :], xb[:, :], ALU.add).then_inc(x2_ready, 1)

            def layernorm2(t):
                newton_rstd(NT + t)
                if not (isinstance(t, int) and t == 0):
                    dve.wait_ge(xn2T_put, t)
                    dve.wait_ge(xn2_stored, 16 * t)
                normalize(xn2[:, :], x2[:, :]).then_inc(xn2_ready, 1)

            def put_scores(t):
                dve.wait_ge(score_put, t + 1)
                s = scores[:, :]
                nc.vector.tensor_tensor(s, pA[:, 0:E], gb_b[:, :], ALU.add).then_inc(score_sum, 1)
                dve.wait_ge(score_sum, t + 1)
                nc.vector.tensor_tensor(s, s, gb2_b[:, :], ALU.add).then_inc(score_ready, 1)
                dve.wait_ge(score_ready, t + 1)
                dve.nop(nofuse=True)
                nc.vector.max(top8[:, :], s).then_inc(top_done, 1)
                dve.wait_ge(top_done, t + 1)
                dve.nop(nofuse=True)
                nc.vector.max_index(topi8[:, :], top8[:, :], s).then_inc(topi_done, 1)
                nc.vector.tensor_copy(top[:, ds(t * E, E)], top8[:, :])
                dve.wait_ge(topi_done, t + 1)
                nc.vector.tensor_copy(topi[:, ds(t * E, E)], topi8[:, :]).then_inc(top_kept, 1)

            for c in range(NC):
                if c >= 1:
                    dve_qsT(c - 1, (c - 1) % 2)
                dve_q(c, c)
            dve_qx(1)
            dve.wait_ge(s_small, 48)

            def dve_tile(t, first, last):
                for c in range(NC):
                    m = 4 * t + c
                    if c == 2:
                        residual(t - 1)
                        dve.wait_ge(x2_ready, t)
                        stats(x2[:, :], NT + t - 1)
                    if c == 3 and not last:
                        dve_qx(t + 1)
                    dve_qsT(m - 1, (c - 1) % 2)
                    dve_q(m, c)
                    if c == 2:
                        layernorm2(t - 1)
                    if c == 0 and not first:
                        put_scores(t - 2)

            dve_tile(1, True, False)
            with dve.Fori(2, NT - 1) as t:
                dve_tile(t, False, False)
            dve_tile(NT - 1, False, True)
            dve_qsT(4 * NT - 1, 1)
            put_scores(NT - 2)
            residual(NT - 1)
            dve.wait_ge(x2_ready, NT)
            stats(x2[:, :], 2 * NT - 1)
            layernorm2(NT - 1)
            put_scores(NT - 1)

            linked = [0]

            def link(ins):
                linked[0] += 1
                ins.then_inc(r_chain, 1)
                dve.wait_ge(r_chain, linked[0])

            def w_lo(k):
                dve.wait_ge(w_hi_ready, k + 1)
                src, rows, dst = w_step(k, w1_lo, w2_lo)
                hi = w_step(k, w1_hi, w2_hi)[2]
                nc.vector.tensor_tensor(dst, src, f(hi), ALU.subtract).then_inc(w_lo_ready, 1)

            v = nc.vector
            row = lambda n: ch[:, n * 32:(n + 1) * 32]
            wide = lambda a, n: a.unsqueeze(2).to_broadcast([P, a.shape[1], n])
            many = lambda a, n: a.unsqueeze(1).to_broadcast([P, n, a.shape[1]])
            by8 = lambda a: a.rearrange("p (n e) -> p n e", e=E)
            top3, topi3 = by8(top[:, :]), by8(topi[:, :])
            dve.wait_ge(top_kept, NT)
            v.tensor_tensor(ch[:, 0:16], top3[:, :, 1], top3[:, :, 0], ALU.subtract).then_inc(gap_ready, 1)
            for c in range(2):
                i = v.tensor_copy(row(1)[:, c * NT:(c + 1) * NT], topi3[:, :, c])
            link(i)
            dve.wait_ge(r_consts, 1)
            link(v.tensor_tensor(by8(hot[:, :]), wide(row(1), E), many(iota_e[:, :], 2 * NT), ALU.is_equal))
            v.memset(mask[:, NT * E:(NT + 1) * E], 0.0)
            v.tensor_tensor(mask[:, 0:NT * E], hot[:, 0:NT * E], hot[:, NT * E:2 * NT * E], ALU.add).then_inc(mask_ready, 1)
            dve.wait_ge(exp_ready, 1)
            link(v.tensor_scalar(ch[:, 0:16], ch[:, 16:32], 1.0, None, ALU.add))
            link(v.reciprocal(row(2)[:, 0:NT], ch[:, 0:16]))
            link(v.tensor_tensor(row(2)[:, NT:2 * NT], ch[:, 16:32], row(2)[:, 0:NT], ALU.mult))
            link(v.tensor_copy(gate_hl[:, 0:32], row(2)))
            link(lo(gate_hl[:, 32:64], row(2), gate_hl[:, 0:32]))
            for k in range(4):
                w_lo(k)
            dve.wait_ge(rank_put, 1)
            n_e = pT[:, NT * E:(NT + 1) * E]
            c16 = cmp[:, 0:E * NT].rearrange("p (e k) -> p e k", e=E)
            link(v.tensor_tensor(c16, wide(n_e, NT), many(k128[:, :], E), ALU.is_gt))
            link(v.tensor_reduce(small[:, 0:E], c16, AX_X, ALU.add))
            link(v.tensor_tensor(by8(cmp[:, 0:E * E]), by8(tri8[:, :]), many(small[:, 0:E], E), ALU.mult))
            link(v.tensor_reduce(small[:, E:2 * E], by8(cmp[:, 0:E * E]), AX_X, ALU.add))
            link(v.tensor_tensor(small[:, 2 * E:3 * E], small[:, E:2 * E], small[:, 0:E], ALU.subtract))
            link(v.tensor_scalar(small[:, 2 * E:3 * E], small[:, 2 * E:3 * E], float(P), None, ALU.mult))
            link(v.tensor_tensor(by8(slot_of[:, :]), by8(pT[:, 0:NT * E]), many(small[:, 2 * E:3 * E], NT), ALU.add))
            for c in range(2):
                i = v.tensor_tensor(prod[:, c * NT * E:(c + 1) * NT * E], hot[:, c * NT * E:(c + 1) * NT * E],
                                    slot_of[:, :], ALU.mult)
            link(i)
            link(v.tensor_reduce(row(3), by8(prod[:, :]), AX_X, ALU.add))
            link(v.tensor_copy(ch_i[:, 0:32], row(3)))
            v.tensor_scalar(ch_i[:, 32:64], ch_i[:, 0:32], P - 1, None, ALU.bitwise_and)
            link(v.tensor_scalar(ch_i[:, 64:96], ch_i[:, 0:32], 7, None, ALU.logical_shift_right))
            v.tensor_copy(row(4), ch_i[:, 32:64])
            link(v.tensor_copy(row(5), ch_i[:, 64:96]))
            sv = slot_val[:, :].rearrange("p (a v j) -> p a v j", v=3, j=TW)
            th = f(slot_val[:, :]).rearrange("p (a v j) -> p a v j", v=3, j=TW)[:, :, 2, :]
            link(v.tensor_tensor(sv[:, :, 2, :], wide(row(5), TW), many(iota_j[:, :], 2 * NT), ALU.is_equal))
            v.tensor_tensor(sv[:, :, 0, :], th, wide(idp[:, :], TW), ALU.mult)
            link(v.tensor_tensor(sv[:, :, 1, :], th, wide(f(gate_hl[:, 0:32]), TW), ALU.mult))
            v.tensor_tensor(sv[:, :, 2, :], th, wide(f(gate_hl[:, 32:64]), TW), ALU.mult).then_inc(vals_ready, 1)
            for a in range(2 * NT):
                if a >= RH:
                    dve.wait_ge(row_hot_used, a - RH + 1)
                v.tensor_scalar(row_hot[:, a % RH * P:(a % RH + 1) * P], iota_r[:, :], row(4)[:, a:a + 1], None,
                                ALU.is_equal).then_inc(row_hot_ready, 1)
            link(v.tensor_tensor(by8(cmp[:, :]), many(small[:, E:2 * E], TW), wide(iota_j[:, :], E), ALU.is_le))
            link(v.tensor_reduce(padt[:, 0:TW], by8(cmp[:, :]), AX_X, ALU.add))
            link(v.tensor_scalar(tile_expert[:, :], padt[:, 0:TW], float(E - 1), None, ALU.min))
            for k in range(4, 7):
                w_lo(k)
            dve.wait_ge(table_ready, 1)
            link(v.tensor_scalar(padt[:, 0:TW], table[:, 0:TW], 0.0, pad[:, :], ALU.is_equal, ALU.mult))
            v.tensor_tensor(slot_gate[:, :], table[:, TW:2 * TW], table[:, 2 * TW:3 * TW], ALU.add)
            v.scalar_tensor_tensor(out=slot_token[:, :], in0=table[:, 0:TW], scalar=-1.0, in1=padt[:, 0:TW],
                                   op0=ALU.add, op1=ALU.add).then_inc(slots_ready, 1)
            for k in range(7, WSTEPS):
                w_lo(k)

            dve.wait_ge(w_put, WSTEPS)
            link(v.memset(hT[96:128, 2 * P:3 * P], 0.0))
            v.memset(hT[96:97, 2 * P:3 * P], 1.0).then_inc(hT_ones, 1)

            def dve_gT(i):
                dve.wait_ge(gT_hi_ready, i + 1)
                lo(gT_lo[:, :], pT[:, :], gT_hi[:, :]).then_inc(gT_lo_ready, 1)

            def dve_hT(i):
                dve.wait_ge(hT_ready, i + 1)
                if not (isinstance(i, int) and i == 0):
                    dve.wait_ge(y_put, i)
                v.tensor_copy(hT_hi[:, :], hT[:, :]).then_inc(hT_hi_ready, 1)
                dve.wait_ge(hT_hi_ready, i + 1)
                lo(hT_lo[:, :], hT[:, :], hT_hi[:, :]).then_inc(hT_lo_ready, 1)

            def dve_y(i, b):
                dve.wait_ge(y_put, i + 1)
                if not (isinstance(i, int) and i < 2):
                    dve.wait_ge(sidx_ready, i)
                v.tensor_scalar(y[:, b * D:(b + 1) * D], pK[:, 512:1024], slot_gate[:, ds(i, 1)], None,
                                ALU.mult).then_inc(y_ready, 1)

            dve_gT(0)
            dve_gT(1)
            dve_hT(0)
            dve_gT(2)
            dve_y(0, 0)
            dve_hT(1)
            with dve.Fori(1, NS // 2) as h:
                for b in range(2):
                    dve_gT(2 * h + (b + 1))
                    dve_y(2 * h + (b - 1), 1 - b)
                    dve_hT(2 * h + b)
            dve_y(NS - 2, 1)
            dve_hT(NS - 1)
            dve_y(NS - 1, 0)

        @block.tensor
        def _(pe):
            def three(dst, lhs, rhs, start, stop):
                nc.tensor.matmul(dst, lhs[0], rhs[0], start=start, stop=False)
                nc.tensor.matmul(dst, lhs[0], rhs[1], start=False, stop=False)
                return nc.tensor.matmul(dst, lhs[1], rhs[0], start=False, stop=stop)

            def two(pair, at, n):
                return (pair[0][:, at:at + n] if isinstance(at, int) else pair[0][:, ds(at, n)],
                        pair[1][:, at:at + n] if isinstance(at, int) else pair[1][:, ds(at, n)])

            pe.wait_ge(ident_ready, 1)
            pe.wait_ge(s_gw, 48)
            for b in range(FB):
                nc.tensor.transpose(pX[:, b * E:(b + 1) * E], gw_in[:, b * P:(b + 1) * P], ident[0:E, 0:E])
            for b in range(HB):
                w = min(P, H - b * P)
                nc.tensor.transpose(pX[0:w, 32 + b * E:32 + (b + 1) * E], b1_in[:, b * P:b * P + w], ident[0:E, 0:E])
            nc.tensor.transpose(pX[:, 64:96], b2_in[:, :], ident[0:32, 0:32]).then_inc(gwT_put, 1)

            def transpose_xn(t, b):
                pe.wait_ge(xn_ready, t + 1)
                if not (isinstance(t, int) and t == 0):
                    pe.wait_ge(xnT_ready, t)
                for i in range(FB):
                    last = nc.tensor.transpose(pT[:, i * P:(i + 1) * P], xn_new[:, b * D + i * P:b * D + (i + 1) * P], ident[:, :])
                last.then_inc(xnT_put, 1)

            def project_k(n, c, b):
                pe.wait_ge(xnT_lo_ready, n + 1)
                if not (isinstance(n, int) and n < 2):
                    pe.wait_ge(k_lo_ready, n - 1)
                for i in range(FB):
                    last = three(pK[:, b * 512:(b + 1) * 512], two((xnT_hi, xnT_lo), b * D + i * P, P),
                                 two((wk_hi, wk_lo), c * (FB * CW) + i * CW, CW), i == 0, i == FB - 1)
                last.then_inc(kproj_done, 1)

            def accumulate_at(n, b, start=False, stop=False):
                pe.wait_ge(xn_lo_ready, n + 1)
                pe.wait_ge(k_lo_ready, n + 1)
                for i in range(FB):
                    last = three(pA[:, i * 512:(i + 1) * 512], two((xn_hi, xn_lo), b * D + i * P, P),
                                 two((k_hi, k_lo), b * CW, CW), start, stop)
                last.then_inc(a_done, 1)

            for t in range(2):
                transpose_xn(t, t)
            pe.wait_ge(wk_lo_ready, 1)
            project_k(0, 0, 0)

            def chunk0_pair(p):
                for b in range(2):
                    n = 2 * p + b
                    if not isinstance(p, int) or p < 7:
                        transpose_xn(n + 2, b)
                    if not isinstance(n, int) or n < NT - 1:
                        project_k(n + 1, 0, 1 - b)
                    accumulate_at(n, b, isinstance(n, int) and n == 0, isinstance(n, int) and n == NT - 1)

            chunk0_pair(0)
            with pe.Fori(1, 7) as p:
                chunk0_pair(p)
            chunk0_pair(7)
            pe.wait_ge(wk_lo_ready, NC)

            def pe_kv(n):
                pe.wait_ge(c_lo_ready, n + 1)
                for i in range(FB):
                    for w in (wv_hi, wv_lo):
                        nc.tensor.matmul(pT[:, 0:256], w[:, i * P:(i + 1) * P], at_hl[:, i * 256:(i + 1) * 256],
                                         start=i == 0 and w is wv_hi, stop=i == FB - 1 and w is wv_lo)
                nc.tensor.matmul(pT[:, 256:512], ones[:, :], ks_hl[:, :], start=True, stop=True).then_inc(kv_put, 1)

            def pe_m(n):
                pe.wait_ge(kv_lo_ready, n + 1)
                three(pX[:, :], (bd_hi[:, :], bd_lo[:, :]), (wo_hi[:, :], wo_lo[:, :]), True, True).then_inc(m_put, 1)

            with pe.Fori(1, NC) as c:
                n0 = c * NT
                project_k(n0, c, 0)
                for j in range(4):
                    for i in range(4):
                        n = n0 + (4 * j + i)
                        if 4 * j + i < NT - 1:
                            project_k(n + 1, c, 1 - i % 2)
                        if j == 0 and i == 0:
                            pe.wait_ge(at_act, c)
                            pe.wait_ge(at_dve, c)
                        accumulate_at(n, i % 2, j == 0 and i == 0, j == 3 and i == 3)
                        if i == 1:
                            pe_kv(4 * c + (j - 4))
                        if i == 2:
                            pe_m(4 * c + (j - 4))
            for j in range(4):
                pe_kv(NP - 4 + j)
                pe_m(NP - 4 + j)

            def project_q(m, t, c, first):
                if c == 0:
                    pe.wait_ge(qx_lo_ready, t + 1)
                if first:
                    pe.wait_ge(wq_lo_ready, c + 1)
                if not (first and c < 2):
                    pe.wait_ge(q_ready, m - 1)
                for i in range(FB):
                    last = three(pK[:, (c % 2) * 512:(c % 2 + 1) * 512], two((qx_hi, qx_lo), i * P, P),
                                 two((wq_hi, wq_lo), c * 2048 + i * CW, CW), i == 0, i == FB - 1)
                last.then_inc(q_put, 1)

            def transpose_qs(m, b):
                pe.wait_ge(qs_ready, m + 1)
                if not (isinstance(m, int) and m < 2):
                    pe.wait_ge(qsT_lo_ready, m - 1)
                for j in range(CB):
                    i = nc.tensor.transpose(pA[:, (2 + b) * 512 + j * P:(2 + b) * 512 + (j + 1) * P],
                                            qs[:, b * CW + j * P:b * CW + (j + 1) * P], ident[:, :])
                i.then_inc(qsT_put, 1)

            def times_m(m, c):
                pe.wait_ge(qsT_lo_ready, m + 1)
                for j in range(CB):
                    last = three(pX[:, :], two((qsT_hi, qsT_lo), (c % 2) * CW + j * P, P),
                                 two((m_hi, m_lo), (c * CB + j) * D, D), c == 0 and j == 0, c == NC - 1 and j == CB - 1)
                last.then_inc(o_put, 1)

            def transpose_xn2(t):
                pe.wait_ge(xn2_ready, t + 1)
                for b in range(FB):
                    i = nc.tensor.transpose(pT[:, b * P:(b + 1) * P], xn2[:, b * P:(b + 1) * P], ident[:, :])
                i.then_inc(xn2T_put, 1)

            def gate(t):
                pe.wait_ge(xn2T_ready, t + 1)
                for b in range(FB):
                    i = nc.tensor.matmul(pA[:, 0:E], xn2T[:, b * P:(b + 1) * P], gwT[:, b * E:(b + 1) * E],
                                         start=b == 0, stop=b == FB - 1)
                i.then_inc(score_put, 1)

            pe.wait_ge(m_lo_ready, 16)
            pe.wait_ge(at_act, NC)
            pe.wait_ge(at_dve, NC)
            for c in range(NC):
                project_q(c, 0, c, True)
                if c >= 1:
                    transpose_qs(c - 1, (c - 1) % 2)
                if c >= 2:
                    times_m(c - 2, c - 2)
            with pe.Fori(1, NT) as t:
                for c in range(NC):
                    m = 4 * t + c
                    project_q(m, t, c, False)
                    if c == 3:
                        transpose_xn2(t - 1)
                    transpose_qs(m - 1, (c - 1) % 2)
                    if c == 2:
                        pe.wait_ge(x2_ready, t)
                    times_m(m - 2, (c - 2) % 4)
                    if c == 3:
                        gate(t - 1)
            transpose_qs(4 * NT - 1, 1)
            times_m(4 * NT - 2, 2)
            times_m(4 * NT - 1, 3)
            transpose_xn2(NT - 1)
            gate(NT - 1)

            def w_transpose(k):
                if k == 0:
                    pe.wait_ge(s_w1a, 16 * 11)
                    pe.wait_ge(score_ready, NT)
                    pe.wait_ge(qsT_lo_ready, NC * NT)
                if k == 11:
                    pe.wait_ge(s_w1b, 16 * 11)
                if k >= 4:
                    pe.wait_ge(w_lo_ready, k - 3)
                bank = (k % 4) * 512
                if k < W1T:
                    for b in range(FB):
                        i = nc.tensor.transpose(pA[:, bank + b * P:bank + (b + 1) * P],
                                                w1_in[k][:, b * P:(b + 1) * P], ident[:, :])
                else:
                    e, hb = divmod(k - W1T, HB)
                    if hb == 0:
                        pe.wait_ge(s_w2[e], 16)
                        pe.wait_ge(b2_put, e + 1)
                    w = min(P, W2C - hb * P)
                    for b in range(FB):
                        i = nc.tensor.transpose(pA[0:w, bank + b * P:bank + (b + 1) * P],
                                                w2_in[e][:, b * W2C + hb * P:b * W2C + hb * P + w], ident[:, :])
                i.then_inc(w_put, 1)

            for k in range(4):
                w_transpose(k)
            pe.wait_ge(mask_ready, 1)
            pe.wait_ge(r_consts, 1)
            nc.tensor.matmul(pT[:, 0:(NT + 1) * E], before[:, :], mask[:, :], start=True, stop=False)
            for t in range(NT):
                n = NT - t
                i = nc.tensor.matmul(pT[:, (t + 1) * E:(NT + 1) * E].rearrange("p (n e) -> p n e", e=E), ones_b[:, :],
                                     mask[:, t * E:(t + 1) * E].unsqueeze(1).to_broadcast([P, n, E]),
                                     start=False, stop=t == NT - 1)
            i.then_inc(rank_put, 1)
            for k in range(4, 7):
                w_transpose(k)
            pe.wait_ge(vals_ready, 1)
            for a in range(2 * NT):
                pe.wait_ge(row_hot_ready, a + 1)
                nc.tensor.matmul(pX[:, 0:3 * TW], row_hot[:, a % RH * P:(a % RH + 1) * P],
                                 slot_val[:, a * 3 * TW:(a + 1) * 3 * TW], start=a == 0,
                                 stop=a == 2 * NT - 1).then_inc(row_hot_used, 1)
            for k in range(7, WSTEPS):
                w_transpose(k)

            def pe_gT(i, b):
                pe.wait_ge(s_g[b], 16 * (i // 2) + 16 if isinstance(i, int) else 8 * i + (16 - 8 * b))
                if not (isinstance(i, int) and i == 0):
                    pe.wait_ge(gT_lo_ready, i)
                for n in range(FB):
                    last = nc.tensor.transpose(pT[:, n * P:(n + 1) * P], xg[:, b * D + n * P:b * D + (n + 1) * P], ident[:, :])
                last.then_inc(gT_put, 1)

            def pe_h(i, e):
                pe.wait_ge(gT_lo_ready, i + 1)
                if not (isinstance(i, int) and i == 0):
                    pe.wait_ge(h_ready, i)
                for n in range(FB):
                    last = three(pK[:, 0:H], two((gT_hi, gT_lo), n * P, P), two((w1_hi, w1_lo), e * H + n * EH, H),
                                 n == 0, n == FB - 1)
                last.then_inc(h_put, 1)

            def pe_hT(i):
                pe.wait_ge(h_ready, i + 1)
                if not (isinstance(i, int) and i == 0):
                    pe.wait_ge(hT_ready, i)
                for n in range(HB):
                    w = min(P, H - n * P)
                    last = nc.tensor.transpose(pX[0:w, n * P:(n + 1) * P], h_in[:, n * P:n * P + w], ident[:, :])
                last.then_inc(hT_put, 1)

            def pe_y(i, e):
                pe.wait_ge(hT_lo_ready, i + 1)
                if not (isinstance(i, int) and i == 0):
                    pe.wait_ge(y_ready, i)
                for n in range(HB):
                    w = min(P, W2C - n * P)
                    hs = (hT_hi[0:w, n * P:(n + 1) * P], hT_lo[0:w, n * P:(n + 1) * P])
                    at_ = e * (HB * D) + n * D
                    last = three(pK[:, 512:1024], hs, (w2_hi[0:w, ds(at_, D)], w2_lo[0:w, ds(at_, D)]),
                                 n == 0, n == HB - 1)
                last.then_inc(y_put, 1)

            def expert(i):
                return pe.value_load(tile_expert[0:1, ds(i, 1)], min_val=0, max_val=E - 1)

            pe.wait_ge(slots_ready, 1)
            pe.wait_ge(w_lo_ready, WSTEPS)
            pe_gT(0, 0)
            pe_h(0, expert(0))
            pe_gT(1, 1)
            pe_hT(0)
            pe_h(1, expert(1))
            pe_gT(2, 0)
            pe_y(0, expert(0))
            pe_hT(1)
            with pe.Fori(1, NS // 2) as h:
                for b in range(2):
                    i = 2 * h + b
                    pe_h(i, expert(i))
                    pe_gT(2 * h + (b + 1), 1 - b)
                    pe_y(2 * h + (b - 1), expert(2 * h + (b - 1)))
                    pe_hT(i)
            pe_h(NS - 1, expert(NS - 1))
            pe_y(NS - 2, expert(NS - 2))
            pe_hT(NS - 1)
            pe_y(NS - 1, expert(NS - 1))


_NAMES = ["attn_hidden_states", "attn_Wq", "attn_Wk", "attn_Wv", "attn_Wo", "attn_bo",
          "ffn_gate_w", "ffn_gate_b", "ffn_bias", "ffn_w1", "ffn_b1", "ffn_w2", "ffn_b2"]


def kernel(**inputs):
    import numpy as np
    import concourse.bacc as bacc
    from concourse.bass_utils import run_bass_kernel_spmd as _run

    nc = bacc.Bacc("TRN2", target_bir_lowering=False, num_devices=1)
    arrays, args = {}, []
    for name in _NAMES:
        a = np.ascontiguousarray(inputs["L0_" + name])
        if name == "attn_hidden_states":
            a = a.reshape(T, D)
        arrays[f"in_{name}"] = a
        args.append(nc.dram_tensor(f"in_{name}", a.shape, F32, kind="ExternalInput").ap())
    args.append(nc.dram_tensor("out", (T + P, D), F32, kind="ExternalOutput").ap())
    block_kernel(nc, *args)
    r = _run(nc, [arrays], core_ids=[0])
    return r.results[0]["out"][:T].reshape(1, T, D)
```

```python
from contextlib import ExitStack

import concourse.bass as bass
from concourse import mybir

F32 = mybir.dt.float32
F32R = mybir.dt.float32r
BF16 = mybir.dt.bfloat16
F16 = mybir.dt.float16
I32 = mybir.dt.int32
U32 = mybir.dt.uint32
ALU = mybir.AluOpType
ACT = mybir.ActivationFunctionType
AX_X = mybir.AxisListType.X
ds = bass.ds

P = 128
T = 2048
D = 512
INNER = 2048
HD = 64
NT = T // P
FB = D // P
CW = 512
NC = INNER // CW
CB = CW // P
HC = CW // HD
NP = INNER // P
E = 8
H = 352
EH = E * H
HB = 3
HR = H - 2 * P
W1T = EH // P
NS = T * 2 // P + E - 1
TW = NS + 1
EPS = 1e-5
KB = 1024
BASE = 16512


def block_kernel(nc, x, Wq, Wk, Wv, Wo, bo, gate_w, gate_b, gbias, w1, b1, w2, b2, out):
    xnT_dram = nc.dram_tensor("xnT_dram", (NT, P, D), F32, kind="Internal").ap()
    xn2_dram = nc.dram_tensor("xn2_dram", (T + P, D), F32, kind="Internal").ap()

    def sb(name, cols, at, dt=F32, parts=P):
        assert at + (2 if dt in (BF16, F16) else 4) * cols <= 229344 - BASE, name
        return nc.alloc_sbuf_tensor_at(name, [parts, cols], dt, offset=BASE + at)

    wk_hi = sb("wk_hi", FB * INNER, 0, F32R)
    wk_lo = sb("wk_lo", FB * INNER, 32 * KB, F32R)
    xn = sb("xn", NT * D, 64 * KB)
    xnT = sb("xnT", NT * D, 96 * KB)
    xnT_hi = sb("xnT_hi", 2 * D, 128 * KB, F32R)
    xnT_lo = sb("xnT_lo", 2 * D, 132 * KB, F32R)
    xn_hi = sb("xn_hi", 2 * D, 136 * KB, F32R)
    xn_lo = sb("xn_lo", 2 * D, 140 * KB, F32R)
    k_hi = sb("k_hi", 2 * CW, 144 * KB, F32R)
    k_lo = sb("k_lo", 2 * CW, 148 * KB, F32R)
    wk_in = sb("wk_in", FB * CW, 152 * KB)
    kacc = sb("kacc", INNER, 160 * KB)
    at = sb("at", FB * CW, 168 * KB)
    xn_new = sb("xn_new", 2 * D, 168 * KB)
    wv_in = sb("wv_in", 2 * D, 176 * KB)
    wo_in = sb("wo_in", 2 * D, 180 * KB)
    wv_hi = sb("wv_hi", D, 184 * KB, F32R)
    wv_lo = sb("wv_lo", D, 186 * KB, F32R)
    wo_hi = sb("wo_hi", D, 188 * KB, F32R)
    wo_lo = sb("wo_lo", D, 190 * KB, F32R)
    at_hl = sb("at_hl", 2 * D, 192 * KB, F32R)
    ks_hl = sb("ks_hl", 2 * P, 196 * KB, F32R)
    part = sb("part", 2 * P, 197 * KB)
    kvT = sb("kvT", P, 198 * KB)
    m_hi = sb("m_hi", 16 * D, 0, F32R)
    m_lo = sb("m_lo", 16 * D, 32 * KB, F32R)
    ksum = sb("ksum", INNER, 160 * KB)
    WQ_HI, WQ_LO = (104, 112, 120, 96), (64, 72, 80, 88)
    wq_hi = [sb(f"wq_hi{c}", FB * CW, WQ_HI[c] * KB, F32R) for c in range(NC)]
    wq_lo = [sb(f"wq_lo{c}", FB * CW, WQ_LO[c] * KB, F32R) for c in range(NC)]
    qsT_hi = sb("qsT_hi", 2 * CW, 136 * KB, F32R)
    qsT_lo = sb("qsT_lo", 2 * CW, 140 * KB, F32R)
    q = sb("q", 2 * CW, 144 * KB)
    qs = sb("qs", 2 * CW, 148 * KB)
    xnT_in = sb("xnT_in", D, 168 * KB)
    x_in = sb("x_in", D, 170 * KB)
    xb = sb("xb", D, 172 * KB)
    x2 = sb("x2", D, 174 * KB)
    xn2 = sb("xn2", D, 176 * KB)
    gprod = [sb("gprod0", D, 178 * KB), sb("gprod1", D, 201 * KB)]
    gw_b = sb("gw_b", 5 * D, 180 * KB)
    gw_late = sb("gw_late", 3 * D, 190 * KB)
    M0 = 200 * KB
    ident = sb("ident", P, M0)
    ones = sb("ones", P, M0 + 512, F32R)
    neg_ident = sb("neg_ident", P, M0 + 512, F32R)
    bd_hi = sb("bd_hi", P, M0 + 1024, F32R)
    bd_lo = sb("bd_lo", P, M0 + 2048, F32R)
    bo_b = sb("bo_b", D, M0 + 3072)
    scores = sb("scores", E, M0 + 5120)
    top8 = sb("top8", E, M0 + 5152)
    topi8 = sb("topi8", E, M0 + 5184, U32)
    gb_b = sb("gb_b", E, M0 + 5760)
    gb2_b = sb("gb2_b", E, M0 + 5792)
    b1_in = sb("b1_in", H, 164 * KB, parts=E)
    b2_in = sb("b2_in", P, 162 * KB, parts=FB * E)
    eps = sb("eps", 1, M0 + 5824)
    warm = sb("warm", 1, M0 + 5632)
    st6 = sb("st6", 6, M0 + 5856)
    mv = sb("mv", 2, M0 + 5888)
    rs = sb("rs", 5, M0 + 5920)
    nrm = sb("nrm", 3 * HC, M0 + 5952)
    top = sb("top", NT * E, M0 + 6048)
    topi = sb("topi", NT * E, M0 + 6560, U32)
    slot_token = sb("slot_token", TW, M0 + 7072, I32)
    slot_gate = sb("slot_gate", TW, M0 + 7232)
    tile_expert = sb("tile_expert", TW, M0 + 7392, I32)
    b1T = sb("b1T", HB * E, M0 + 7552)
    gidx = sb("gidx", 2, M0 + 7648, I32)
    sidx = sb("sidx", 2, M0 + 7680, I32)
    b2T = sb("b2T", FB * E, M0 + 7712)
    zero = sb("zero", D, 198 * KB)
    w1_hi = sb("w1_hi", FB * EH, 0, F32R)
    w1_lo = sb("w1_lo", FB * EH, 44 * KB, F32R)
    w2_hi = sb("w2_hi", E * HB * D, 88 * KB, F32R)
    w2_lo = sb("w2_lo", E * HB * D, 136 * KB, F32R)
    w1_at = [(n * KB) for n in (152, 154, 156, 158, 190, 192, 194, *range(104, 122, 2), 134, 136, 182, 184, 186, 188)]
    w1_in = [sb(f"w1_in{k}", D, w1_at[k]) for k in range(W1T)]
    W2C = H + 1
    w2_at = [156 * KB, 156 * KB + 5664, 156 * KB + 2 * 5664, 156 * KB + 3 * 5664, 122 * KB, 122 * KB + 5664,
             184 * KB, 184 * KB + 5664]
    w2_in = [sb(f"w2_in{e}", FB * W2C, w2_at[e]) for e in range(E)]
    slot_val = sb("slot_val", 2 * NT * 3 * TW, 88 * KB, F32R)
    hot = sb("hot", 2 * NT * E, 103 * KB)
    RH = 8
    row_hots = [sb(f"row_hot{i}", 4 * P, at, F32R) for i, at in enumerate((M0 + 1024, 150 * KB))]
    row_hot = lambda a: row_hots[a % RH // 4][:, a % 4 * P:(a % 4 + 1) * P]
    slot_of = sb("slot_of", NT * E, M0 + 3072)
    prod = sb("prod", 2 * NT * E, M0 + 3584)
    mask = sb("mask", (NT + 1) * E, M0 + 4608, BF16)
    R1 = 138 * KB
    ch = sb("ch", 9 * 32, R1)
    ch_i = sb("ch_i", 3 * 32, R1 + 1152, I32)
    gate_hl = sb("gate_hl", 2 * 32, R1 + 1536, F32R)
    w_raw = [sb(f"w_raw{i}", D, (142 + 2 * i) * KB if i < 4 else M0 + 1024 + 2048 * (i - 4)) for i in range(6)]
    R2 = 196 * KB
    iota_e = sb("iota_e", E, R2)
    iota_j = sb("iota_j", TW, R2 + 32)
    k128 = sb("k128", NT, R2 + 192)
    tri8 = sb("tri8", E * E, R2 + 256)
    pad = sb("pad", 1, R2 + 512)
    iota_r = sb("iota_r", P, R2 + 544, F16)
    idp = sb("idp", 2 * NT, R2 + 800, F16)
    before = sb("before", P, R2 + 864, BF16)
    ones_b = sb("ones_b", P, R2 + 1120, BF16)
    cmp = sb("cmp", TW * E, R2 + 1536)
    small = sb("small", 4 * E, R2 + 2816)
    table = sb("table", 3 * TW, R2 + 2944)
    padt = sb("padt", TW, R2 + 3424)
    iota32 = sb("iota32", TW, R2 + 1536, I32)
    iota_r32 = sb("iota_r32", P, R2 + 2048, I32)
    gT_hi = sb("gT_hi", D, 184 * KB, F32R)
    gT_lo = sb("gT_lo", D, 186 * KB, F32R)
    h_in = sb("h_in", H, 188 * KB)
    hT = sb("hT", HB * P, 188 * KB + 1408)
    hT_hi = sb("hT_hi", HB * P, 190 * KB + 896, F32R)
    hT_lo = sb("hT_lo", HB * P, 192 * KB + 384, F32R)
    xg = sb("xg", 2 * D, 196 * KB)
    y = sb("y", 2 * D, M0 + 1024)

    with ExitStack() as ctx:
        def pb(name, n=1):
            return ctx.enter_context(nc.psum_tensor(name, [P, n * 512], F32))

        def sem(name):
            return ctx.enter_context(nc.semaphore(name))

        pA = pb("pA", 4)
        pK = pb("pK", 2)
        pT = pb("pT", 1)
        pX = pb("pX", 1)

        s_first = sem("s_first")
        s_x = [sem(f"s_x{i}") for i in range(4)]
        s_b = sem("s_b")
        s_gw = sem("s_gw")
        gw_put = sem("gw_put")
        s_wk = sem("s_wk")
        s_small = sem("s_small")
        s_wv = [sem(f"s_wv{i}") for i in range(2)]
        s_wq = [sem(f"s_wq{i}") for i in range(NC)]
        xnT_stored = sem("xnT_stored")
        ident_ready = sem("ident_ready")
        pool_own = sem("pool_own")
        pool_link = sem("pool_link")
        consts_ready = sem("consts_ready")
        bT_put = sem("bT_put")
        bT_ready = sem("bT_ready")
        bn_stats_done = sem("bn_stats_done")
        rstd_step = sem("rstd_step")
        qk_ready = sem("qk_ready")
        nsum_ready = sem("nsum_ready")
        nclip_ready = sem("nclip_ready")
        nrec_ready = sem("nrec_ready")
        score_sum = sem("score_sum")
        var_ready = sem("var_ready")
        sqrt_ready = sem("sqrt_ready")
        xn_ready = sem("xn_ready")
        xn_kept = sem("xn_kept")
        xnT_put = sem("xnT_put")
        xnT_ready = sem("xnT_ready")
        xnT_hi_ready = sem("xnT_hi_ready")
        xnT_lo_ready = sem("xnT_lo_ready")
        xn_hi_ready = sem("xn_hi_ready")
        xn_lo_ready = sem("xn_lo_ready")
        wk_hi_ready = sem("wk_hi_ready")
        wk_lo_ready = sem("wk_lo_ready")
        kproj_done = sem("kproj_done")
        k_hi_ready = sem("k_hi_ready")
        k_lo_ready = sem("k_lo_ready")
        a_done = sem("a_done")
        kacc_done = sem("kacc_done")
        at_act = sem("at_act")
        at_dve = sem("at_dve")

        operands_hi = sem("operands_hi")
        operands_lo = sem("operands_lo")
        c_hi_ready = sem("c_hi_ready")
        c_lo_ready = sem("c_lo_ready")
        kv_put = sem("kv_put")
        part_ready = sem("part_ready")
        kv_ready = sem("kv_ready")
        kv_hi_ready = sem("kv_hi_ready")
        kv_lo_ready = sem("kv_lo_ready")
        m_put = sem("m_put")
        m_hi_ready = sem("m_hi_ready")
        m_lo_ready = sem("m_lo_ready")

        wq_hi_ready = sem("wq_hi_ready")
        wq_lo_ready = sem("wq_lo_ready")
        s_xnTin = sem("s_xnTin")
        q_put = sem("q_put")
        q_ready = sem("q_ready")
        qs_ready = sem("qs_ready")
        qsT_put = sem("qsT_put")
        qsT_hi_ready = sem("qsT_hi_ready")
        qsT_lo_ready = sem("qsT_lo_ready")
        o_put = sem("o_put")
        s_xin = sem("s_xin")
        xb_ready = sem("xb_ready")
        x2_ready = sem("x2_ready")
        x2_stored = sem("x2_stored")
        xn2_ready = sem("xn2_ready")
        xn2_stored = sem("xn2_stored")
        dots_done = sem("dots_done")
        score_ready = sem("score_ready")
        dump_stored = sem("dump_stored")
        zero_ready = sem("zero_ready")
        r_consts = sem("r_consts")
        top_done = sem("top_done")
        topi_done = sem("topi_done")
        top_kept = sem("top_kept")
        s_w1a = sem("s_w1a")
        s_w1b = sem("s_w1b")
        s_w1c = sem("s_w1c")
        s_w2 = [sem(f"s_w2{e}") for e in range(E)]
        b2_put = sem("b2_put")
        w_put = sem("w_put")
        w_hi_ready = sem("w_hi_ready")
        w_lo_ready = sem("w_lo_ready")
        w_raw_ready = sem("w_raw_ready")
        neg_ready = sem("neg_ready")
        w_sub_put = sem("w_sub_put")
        w_act_ready = sem("w_act_ready")
        w_pool_ready = sem("w_pool_ready")
        row_hot2_ready = sem("row_hot2_ready")
        r_chain = sem("r_chain")
        gap_ready = sem("gap_ready")
        exp_ready = sem("exp_ready")
        mask_ready = sem("mask_ready")
        rank_put = sem("rank_put")
        rows_ready = sem("rows_ready")
        tile_hot_ready = sem("tile_hot_ready")
        tokens_ready = sem("tokens_ready")
        vals_ready = sem("vals_ready")
        row_hot_ready = sem("row_hot_ready")
        row_hot_used = sem("row_hot_used")
        table_ready = sem("table_ready")
        slots_ready = sem("slots_ready")
        hT_ones = sem("hT_ones")
        s_g = [sem(f"s_g{i}") for i in range(2)]
        s_add = sem("s_add")
        gidx_ready = sem("gidx_ready")
        sidx_ready = sem("sidx_ready")
        gT_put = sem("gT_put")
        gT_hi_ready = sem("gT_hi_ready")
        gT_lo_ready = sem("gT_lo_ready")
        h_put = sem("h_put")
        h_ready = sem("h_ready")
        hT_put = sem("hT_put")
        hT_ready = sem("hT_ready")
        hT_hi_ready = sem("hT_hi_ready")
        hT_lo_ready = sem("hT_lo_ready")
        y_put = sem("y_put")
        y_ready = sem("y_ready")

        w1_rows = w1.rearrange("e h d -> (e h) d")
        WSTEPS = W1T + E * HB

        w_bank = lambda k: (pA, pA, pK, pK)[k % 4][:, (2, 3, 0, 1)[k % 4] * 512:((2, 3, 0, 1)[k % 4] + 1) * 512]
        lo_bank = lambda k: pA[:, k % 2 * 512:(k % 2 + 1) * 512]
        PE_STEPS = list(range(12, W1T))
        POOL_STEPS = [k for k in range(WSTEPS) if k < 12 or k >= W1T and k % 7 == 1]
        DVE_STEPS = [k for k in range(WSTEPS) if k not in POOL_STEPS and k not in PE_STEPS]
        first_late = len([k for k in POOL_STEPS if k < W1T])
        raw = lambda k: w_raw[POOL_STEPS.index(k) % 4] if k < W1T else w_raw[4 + (POOL_STEPS.index(k) - first_late) % 2]

        def w_step(k, w1_to, w2_to, bank):
            if k < W1T:
                return bank.rearrange("p (f n) -> p f n", f=FB), P, \
                    w1_to[:, :].rearrange("p (f n) -> p f n", f=FB)[:, :, k * P:(k + 1) * P]
            w = min(P, W2C - (k - W1T) % HB * P)
            return bank[0:w], w, w2_to[0:w, (k - W1T) * D:(k - W1T + 1) * D]

        WQ_SPLIT = ((2, 1), (2, 3), (3, 1), (3, 2))

        def start_q(project, pair, kv, m, put_q, put_qsT, split_wq, times):
            n = NP - 4
            project(0)
            pair(n)
            put_q(0)
            kv(n)
            project(1)
            split_wq(2)
            put_q(1)
            m(n)
            pair(n + 1)
            put_qsT(0)
            project(2)
            kv(n + 1)
            put_q(2)
            m(n + 1)
            pair(n + 2)
            times(0)
            put_qsT(1)
            kv(n + 2)
            split_wq(3)
            times(1)
            m(n + 2)
            pair(n + 3)
            project(3)
            put_qsT(2)
            kv(n + 3)
            put_q(3)
            m(n + 3)

        block = ctx.enter_context(nc.Block())
        f = lambda a: a.bitcast(F32)
        wide = lambda a, n: a.unsqueeze(2).to_broadcast([P, a.shape[1], n])
        sv = slot_val[:, :].rearrange("p (a v j) -> p a v j", v=3, j=TW)
        th = f(slot_val[:, :]).rearrange("p (a v j) -> p a v j", v=3, j=TW)[:, :, 2, :]
        row = lambda n: ch[:, n * 32:(n + 1) * 32]
        blocks = lambda a: a[:, :].rearrange("p (f n) -> p f n", f=FB)
        gw_bank = (pA[:, 0:512], pA[:, 512:1024], pT[:, :])
        m_bank = lambda n: pA[:, 0:512] if isinstance(n, int) and n >= NP - 4 else pX[:, :]
        halves = lambda a: a[:, :].rearrange("p (a n) -> p a n", a=2)

        @block.sync
        def _(sp):
            def load_wk(c):
                sp.dma_start(wk_in[:, :].rearrange("p (f n) -> p f n", f=FB),
                             Wk[:, c * CW:(c + 1) * CW].rearrange("(f p) n -> p f n", p=P)).then_inc(s_wk, 16)

            for g in range(4):
                for t in range(4 * g, 4 * g + 4):
                    sp.dma_start(xn[:, t * D:(t + 1) * D], x[t * P:(t + 1) * P, :]).then_inc(s_x[g] if t else s_first, 16)
                    if t == 0:
                        load_wk(0)
                if g == 0:
                    sp.dma_start(b1_in[:, :], b1).then_inc(s_b, 16)
                    sp.dma_start(b2_in[:, :], b2.rearrange("e (f n) -> (e f) n", n=P)).then_inc(s_b, 16)
            sp.dma_start(bo_b[:, :], bo.partition_broadcast(P)).then_inc(s_small, 16)
            sp.dma_start(gb_b[:, :], gate_b.partition_broadcast(P)).then_inc(s_small, 16)
            sp.dma_start(gb2_b[:, :], gbias.partition_broadcast(P)).then_inc(s_small, 16)
            for c in range(1, NC):
                sp.wait_ge(wk_hi_ready, c)
                sp.wait_ge(wk_lo_ready, c)
                load_wk(c)
            def load_wq(c):
                sp.dma_start(wk_in[:, :].rearrange("p (f n) -> p f n", f=FB),
                             Wq[:, c * CW:(c + 1) * CW].rearrange("(f p) n -> p f n", p=P)).then_inc(s_wq[c], 16)

            def load_pair(n, b):
                sp.dma_start(wv_in[:, b * D:(b + 1) * D].rearrange("p (f n) -> p f n", f=FB),
                             Wv[:, ds(n * P, P)].rearrange("(f p) n -> p f n", p=P)).then_inc(s_wv[b], 16)
                sp.dma_start(wo_in[:, b * D:(b + 1) * D], Wo[ds(n * P, P), :]).then_inc(s_wv[b], 16)

            load_pair(0, 0)
            load_pair(1, 1)
            sp.wait_ge(wk_hi_ready, NC)
            sp.wait_ge(wk_lo_ready, NC)
            load_wq(0)
            sp.wait_ge(xnT_ready, NT)
            for g in range(4):
                sp.dma_start(xnT_dram[4 * g:4 * g + 4].rearrange("t p n -> p t n"),
                             xnT[:, 4 * g * D:4 * (g + 1) * D].rearrange("p (t n) -> p t n", t=4)
                             ).then_inc(xnT_stored, 16)

            with sp.Fori(1, NP // 2 - 2) as h:
                for b in range(2):
                    sp.wait_ge(c_lo_ready, 2 * h + (b - 1))
                    load_pair(2 * h + b, b)
            for n in range(NP - 4, NP):
                sp.wait_ge(c_lo_ready, n - 1)
                if n - 2 >= NP - 4:
                    sp.wait_ge(operands_lo, n - 2 - (NP - 4) + 1)
                load_pair(n, n % 2)
                c = n - (NP - 4) + 1
                if c < NC:
                    sp.wait_ge(wq_hi_ready, 2 * c)
                    sp.wait_ge(wq_lo_ready, 2 * c)
                    load_wq(c)

            sp.wait_ge(m_put, NP)
            sp.wait_ge(m_lo_ready, NP)
            sp.wait_ge(xnT_stored, 64)
            sp.dma_start(xnT_in[:, :], xnT_dram[2]).then_inc(s_xnTin, 16)
            sp.dma_start(x_in[:, :], x[0:P, :]).then_inc(s_xin, 16)
            sp.wait_ge(zero_ready, 1)
            sp.dma_start(out[T:T + P, :], zero[:, :]).then_inc(dump_stored, 16)
            sp.dma_start(xn2_dram[T:T + P, :], zero[:, :]).then_inc(dump_stored, 16)
            def load_w1(first, last, s_w1):
                for k in range(first, last):
                    sp.dma_start(w1_in[k][:, :], w1_rows[k * P:(k + 1) * P, :]).then_inc(s_w1, 16)

            gw_rows = gate_w.rearrange("e d -> (e d)")
            sp.dma_start(gw_late[:, :], gw_rows[5 * D:].partition_broadcast(P)).then_inc(s_gw, 16)
            sp.dma_start(gw_b[:, :], gw_rows[0:5 * D].partition_broadcast(P)).then_inc(s_gw, 16)
            sp.wait_ge(wq_lo_ready, 2 * NC)
            load_w1(0, 4, s_w1a)
            sp.wait_ge(xb_ready, 1)
            sp.dma_start(x_in[:, :], x[P:2 * P, :]).then_inc(s_xin, 16)

            def tile_io(t):
                sp.wait_ge(xnT_hi_ready, t + (NC * NT + 2))
                sp.wait_ge(xnT_lo_ready, t + (NC * NT + 2))
                if not isinstance(t, int) or t + 2 < NT:
                    sp.dma_start(xnT_in[:, :], xnT_dram[ds(t + 2, 1)].rearrange("a p n -> (a p) n")).then_inc(s_xnTin, 16)
                sp.wait_ge(x2_ready, t)
                sp.dma_start(out[ds((t - 1) * P, P), :], x2[:, :]).then_inc(x2_stored, 16)
                sp.wait_ge(xb_ready, t + 1)
                sp.dma_start(x_in[:, :], x[ds((t + 1) * P, P), :]).then_inc(s_xin, 16)
                sp.wait_ge(xn2_ready, t)
                sp.dma_start(xn2_dram[ds((t - 1) * P, P), :], xn2[:, :]).then_inc(xn2_stored, 16)

            tile_io(1)
            sp.wait_ge(gw_put, 1)
            load_w1(4, 7, s_w1a)
            with sp.Fori(2, NT - 2) as t:
                tile_io(t)
            tile_io(NT - 2)
            sp.wait_ge(q_put, NC * NT - 3)
            load_w1(7, 11, s_w1b)
            sp.wait_ge(q_put, NC * NT - 2)
            load_w1(11, 15, s_w1b)
            sp.wait_ge(x2_ready, NT - 1)
            sp.dma_start(out[(NT - 2) * P:(NT - 1) * P, :], x2[:, :]).then_inc(x2_stored, 16)
            sp.wait_ge(xn2_ready, NT - 1)
            sp.dma_start(xn2_dram[(NT - 2) * P:(NT - 1) * P, :], xn2[:, :]).then_inc(xn2_stored, 16)
            sp.wait_ge(q_put, NC * NT - 1)
            load_w1(15, 16, s_w1b)
            sp.wait_ge(q_put, NC * NT)
            sp.wait_ge(x2_ready, NT)
            sp.dma_start(out[(NT - 1) * P:NT * P, :], x2[:, :]).then_inc(x2_stored, 16)
            sp.wait_ge(xn2_ready, NT)
            sp.dma_start(xn2_dram[(NT - 1) * P:NT * P, :], xn2[:, :]).then_inc(xn2_stored, 16)

            def load_w2(e):
                sp.dma_start(w2_in[e][:, :].rearrange("p (f n) -> p f n", f=FB)[:, :, 0:H],
                             w2[e].rearrange("(f p) n -> p f n", p=P)).then_inc(s_w2[e], 16)

            load_w1(16, 18, s_w1c)
            sp.wait_ge(dots_done, E * NT)
            load_w1(18, W1T, s_w1c)
            sp.wait_ge(w_put, 4)
            sp.wait_ge(x2_stored, 16 * NT)
            sp.wait_ge(xn2_stored, 16 * NT)
            for e in range(6):
                load_w2(e)
            sp.wait_ge(w_put, W1T)
            sp.wait_ge(w_sub_put, len(PE_STEPS))
            for e in range(6, E):
                load_w2(e)
            sp.wait_ge(s_add, 16 * NS)
            sp.wait_ge(x2_stored, 16 * NT)
            sp.wait_ge(dump_stored, 32)

        @block.gpsimd
        def _(pool):
            pool.memset(ident[:, :], 1.0).then_inc(pool_own, 1)
            pool.wait_ge(pool_own, 1)
            pool.affine_select(ident[:, :], ident[:, :], pattern=[[-1, P]], base=0, channel_multiplier=1,
                               compare_op=ALU.is_equal, fill=0.0).then_inc(ident_ready, 1)
            pool.memset(eps[:, :], EPS).then_inc(consts_ready, 1)
            pool.memset(f(ones[:, :]), 1.0).then_inc(consts_ready, 1)
            pool.memset(f(bd_hi[:, :]), 0.0).then_inc(consts_ready, 1)
            pool.memset(f(bd_lo[:, :]), 0.0).then_inc(consts_ready, 1)

            linked = [0]

            def link(ins):
                linked[0] += 1
                ins.then_inc(pool_link, 1)
                pool.wait_ge(pool_link, linked[0])

            def add_k(c, n, b):
                acc = kacc[:, ds(c * CW, CW)]
                pool.wait_ge(k_hi_ready, n + 1)
                if not (isinstance(n, int) and n == 0):
                    pool.wait_ge(kacc_done, n)
                pool.nop(nofuse=True)
                pool.tensor_tensor(acc, acc, f(k_hi[:, b * CW:(b + 1) * CW]), ALU.add).then_inc(pool_own, 1)
                pool.wait_ge(pool_own, n + 2)
                pool.wait_ge(k_lo_ready, n + 1)
                pool.nop(nofuse=True)
                pool.tensor_tensor(acc, acc, f(k_lo[:, b * CW:(b + 1) * CW]), ALU.add).then_inc(kacc_done, 1)

            def keep_xn(t, b):
                pool.wait_ge(xn_ready, t + 1)
                pool.tensor_copy(xn[:, ds(t * D, D)], xn_new[:, b * D:(b + 1) * D]).then_inc(xn_kept, 1)

            keep_xn(0, 0)
            keep_xn(1, 1)
            pool.wait_ge(bT_ready, 1)
            pool.memset(kacc[:, :], 0.0).then_inc(consts_ready, 1)
            pool.wait_ge(consts_ready, 5)
            keep_xn(2, 0)
            keep_xn(3, 1)
            for b in range(2):
                keep_xn(4 + b, b)
                add_k(0, b, b)
            with pool.Fori(1, NT // 2 - 2) as p:
                for b in range(2):
                    keep_xn(2 * p + (4 + b), b)
                    add_k(0, 2 * p + b, b)
            with pool.Fori(NT // 2 - 2, NT // 2) as p:
                for b in range(2):
                    add_k(0, 2 * p + b, b)
            with pool.Fori(1, NC) as c:
                with pool.Fori(0, NT // 2) as p:
                    for b in range(2):
                        add_k(c, c * NT + 2 * p + b, b)

            def pool_operands(n):
                b = n % 2
                pool.wait_ge(operands_hi, n + 1)
                pool.tensor_tensor(wv_lo[:, :], wv_in[:, b * D:(b + 1) * D], f(wv_hi[:, :]), ALU.subtract)
                pool.tensor_tensor(wo_lo[:, :], wo_in[:, b * D:(b + 1) * D], f(wo_hi[:, :]), ALU.subtract
                                   ).then_inc(operands_lo, 1)

            for n in range(NP - 4, NP - 1):
                pool_operands(n)
            pool_operands(NP - 1)

            pool.wait_ge(m_lo_ready, NP)
            pool.wait_ge(m_put, NP)
            pool.memset(zero[:, :], 0.0).then_inc(zero_ready, 1)
            link(pool.iota(iota32[:, 0:E], pattern=[[1, E]], base=0, channel_multiplier=0))
            link(pool.tensor_copy(iota_e[:, :], iota32[:, 0:E]))
            link(pool.iota(iota32[:, 0:TW], pattern=[[1, TW]], base=0, channel_multiplier=0))
            link(pool.tensor_copy(iota_j[:, :], iota32[:, 0:TW]))
            link(pool.iota(iota32[:, 0:NT], pattern=[[P, NT]], base=0, channel_multiplier=0))
            link(pool.tensor_copy(k128[:, :], iota32[:, 0:NT]))
            link(pool.iota(iota32[:, 0:1], pattern=[[1, 1]], base=T + 1, channel_multiplier=1))
            link(pool.tensor_copy(pad[:, :], iota32[:, 0:1]))
            link(pool.iota(iota32[:, 0:2 * NT], pattern=[[0, 2], [P, NT]], base=1, channel_multiplier=1))
            link(pool.tensor_copy(idp[:, :], iota32[:, 0:2 * NT]))
            link(pool.memset(tri8[:, :], 1.0))
            link(pool.affine_select(tri8[:, :].rearrange("p (a b) -> p a b", a=E), tri8[:, :].rearrange("p (a b) -> p a b", a=E),
                                    pattern=[[1, E], [-1, E]], base=0, channel_multiplier=0,
                                    compare_op=ALU.is_ge, fill=0.0))
            link(pool.memset(ones_b[:, :], 1.0))
            link(pool.affine_select(before[:, :], ones_b[:, :], pattern=[[1, P]], base=0, channel_multiplier=-1,
                                    compare_op=ALU.is_gt, fill=0.0))
            pool.wait_ge(dump_stored, 32)
            link(pool.iota(iota_r32[:, :], pattern=[[1, P]], base=0, channel_multiplier=0))
            pool.tensor_copy(iota_r[:, :], iota_r32[:, :]).then_inc(r_consts, 1)

            pool.wait_ge(s_small, 16 * 3)
            pool.wait_ge(s_xin, 16)
            pool.tensor_tensor(xb[:, :], x_in[:, :], bo_b[:, :], ALU.add).then_inc(xb_ready, 1)
            with pool.Fori(1, NT) as t:
                pool.wait_ge(s_xin, 16 * t + 16)
                pool.wait_ge(x2_ready, t)
                pool.tensor_tensor(xb[:, :], x_in[:, :], bo_b[:, :], ALU.add).then_inc(xb_ready, 1)

            def gather(i, b, first=False):
                if not first:
                    pool.wait_ge(gT_put, i - 1)
                pool.tensor_copy(gidx[:, b:b + 1], slot_token[:, ds(i, 1)]).then_inc(gidx_ready, 1)
                pool.wait_ge(gidx_ready, i + 1)
                pool.nop(nofuse=True)
                pool.indirect_dma_start(xg[:, b * D:(b + 1) * D], None, xn2_dram,
                                        bass.IndirectOffsetOnAxis(gidx[:, b:b + 1].bitcast(U32), 0)).then_inc(s_g[b], 16)

            def add_out(i, b, first=False):
                if not first:
                    pool.wait_ge(s_add, 16 * i)
                pool.wait_ge(y_ready, i + 1)
                pool.tensor_copy(sidx[:, b:b + 1], slot_token[:, ds(i, 1)]).then_inc(sidx_ready, 1)
                pool.wait_ge(sidx_ready, i + 1)
                pool.nop(nofuse=True)
                pool.indirect_dma_start(out, bass.IndirectOffsetOnAxis(sidx[:, b:b + 1].bitcast(U32), 0),
                                        y[:, b * D:(b + 1) * D], None, compute_op=ALU.add).then_inc(s_add, 16)

            def put_b2(e):
                pool.tensor_copy(w2_in[e][:, :].rearrange("p (f n) -> p f n", f=FB)[:, :, H:H + 1],
                                 b2T[:, e * FB:(e + 1) * FB].unsqueeze(2)).then_inc(b2_put, 1)

            def pool_lo(k):
                pool.wait_ge(w_raw_ready, POOL_STEPS.index(k) + 1)
                src, rows, dst = w_step(k, w1_lo, w2_lo, raw(k))
                hi = w_step(k, w1_hi, w2_hi, raw(k))[2]
                pool.tensor_tensor(dst, src, f(hi), ALU.subtract).then_inc(w_pool_ready, 1)

            for k in POOL_STEPS[:12]:
                pool_lo(k)
            pool.wait_ge(tile_hot_ready, 1)
            pool.tensor_tensor(sv[:, :, 0, :], th, wide(idp[:, :], TW), ALU.mult).then_inc(tokens_ready, 1)
            pool.wait_ge(rows_ready, 1)
            for a in range(3, 2 * NT, 4):
                if a >= RH:
                    pool.wait_ge(row_hot_used, a - RH + 1)
                pool.tensor_scalar(row_hot(a), iota_r[:, :], row(4)[:, a:a + 1], None,
                                   ALU.is_equal).then_inc(row_hot2_ready, 1)
            pool.wait_ge(x2_ready, NT)
            pool.wait_ge(qs_ready, NC * NT)
            pool.wait_ge(o_put, NC * NT)
            pool.wait_ge(x2_stored, 16 * NT)
            pool.wait_ge(xn2_stored, 16 * NT)
            pool.wait_ge(dots_done, E * NT)
            for e in range(6):
                put_b2(e)
            for k in POOL_STEPS[12:]:
                if k == POOL_STEPS[first_late]:
                    pool.wait_ge(w_put, W1T)
                    pool.wait_ge(w_sub_put, len(PE_STEPS))
                    put_b2(6)
                    put_b2(7)
                    pool.wait_ge(slots_ready, 1)
                    gather(0, 0, True)
                    gather(1, 1, True)
                pool_lo(k)

            gather(2, 0)
            gather(3, 1)
            add_out(0, 0, True)
            with pool.Fori(1, NS // 2 - 1) as h:
                for b in range(2):
                    gather(2 * h + (b + 2), b)
                    add_out(2 * h + (b - 1), 1 - b)
            gather(NS - 1, 0)
            for i in range(NS - 4, NS):
                add_out(i, i % 2)

        @block.scalar
        def _(act):
            def split_wk(c):
                act.wait_ge(s_wk, 16 * c + 16)
                for b in range(FB):
                    i = nc.scalar.copy(wk_hi[:, (c * FB + b) * CW:(c * FB + b + 1) * CW],
                                       wk_in[:, b * CW:(b + 1) * CW])
                i.then_inc(wk_hi_ready, 1)

            def sqrt_var(t):
                act.wait_ge(var_ready, t + 1)
                nc.scalar.activation(rs[:, 0:1], mv[:, 1:2], ACT.Sqrt, bias=eps[:, :]).then_inc(sqrt_ready, 1)

            def put_xnT(t):
                act.wait_ge(xnT_put, t + 1)
                nc.scalar.copy(xnT[:, ds(t * D, D)], pT[:, :]).then_inc(xnT_ready, 1)

            def split_xnT(n, t, b):
                if isinstance(n, int) and n < 2:
                    act.wait_ge(xnT_ready, n + 1)
                else:
                    act.wait_ge(kproj_done, n - 1)
                    act.nop(nofuse=True)
                nc.scalar.copy(xnT_hi[:, b * D:(b + 1) * D], xnT[:, ds(t * D, D)]).then_inc(xnT_hi_ready, 1)

            def split_xn(n, t, b):
                if not (isinstance(n, int) and n < 2):
                    act.wait_ge(a_done, n - 1)
                nc.scalar.copy(xn_hi[:, b * D:(b + 1) * D], xn[:, ds(t * D, D)]).then_inc(xn_hi_ready, 1)

            def split_k(n, b):
                act.wait_ge(kproj_done, n + 1)
                if not (isinstance(n, int) and n < 2):
                    act.wait_ge(a_done, n - 1)
                    act.wait_ge(kacc_done, n - 1)
                nc.scalar.activation(k_hi[:, b * CW:(b + 1) * CW], pK[:, b * 512:(b + 1) * 512],
                                     ACT.Relu).then_inc(k_hi_ready, 1)

            def put_at(c):
                act.wait_ge(a_done, c * NT + NT)
                for b in range(2):
                    i = nc.scalar.copy(at[:, b * CW:(b + 1) * CW], pA[:, b * 512:(b + 1) * 512])
                i.then_inc(at_act, 1)

            act.wait_ge(consts_ready, 1)
            nc.scalar.activation(warm[:, :], eps[:, :], ACT.Sqrt)
            sqrt_var(0)
            sqrt_var(1)
            split_wk(0)
            for t in range(2):
                put_xnT(t)
                split_xnT(t, t, t)
                sqrt_var(t + 2)
            act.wait_ge(bT_put, 1)
            nc.scalar.copy(b1T[:, 0:2 * E], pX[:, 32:32 + 2 * E])
            nc.scalar.copy(b1T[0:HR, 2 * E:3 * E], pX[0:HR, 32 + 2 * E:32 + 3 * E])
            nc.scalar.copy(b2T[:, :], pX[:, 64:96]).then_inc(bT_ready, 1)
            act.wait_ge(xn_kept, 1)
            split_xn(0, 0, 0)

            def chunk0_pair(p):
                for b in range(2):
                    n = 2 * p + b
                    if not isinstance(p, int) or p < 6:
                        sqrt_var(n + 4)
                    if not isinstance(p, int) or p < 7:
                        put_xnT(n + 2)
                    split_k(n, b)
                    if not isinstance(p, int) or p < 7:
                        act.wait_ge(xnT_ready, n + 3)
                        split_xnT(n + 2, n + 2, b)
                        act.wait_ge(xn_kept, n + 2)
                    else:
                        split_xnT(n + 2, b, b)
                    split_xn(n + 1, (n + 1) % NT if isinstance(p, int) else n + 1, 1 - b)

            chunk0_pair(0)
            with act.Fori(1, 6) as p:
                chunk0_pair(p)
            split_wk(1)
            chunk0_pair(6)
            split_wk(2)
            chunk0_pair(7)
            put_at(0)
            split_wk(3)

            def act_operands(n, b, loads):
                act.wait_ge(s_wv[b], loads)
                nc.scalar.copy(wv_hi[:, :], wv_in[:, b * D:(b + 1) * D])
                nc.scalar.copy(wo_hi[:, :], wo_in[:, b * D:(b + 1) * D]).then_inc(operands_hi, 1)

            def act_pair(n, j):
                nc.scalar.copy(blocks(at_hl)[:, :, 0:P], blocks(at)[:, :, j * P:(j + 1) * P])
                nc.scalar.copy(ks_hl[:, 0:P], kacc[:, ds(n * P, P)]).then_inc(c_hi_ready, 1)

            def act_kv(n):
                act.wait_ge(kv_put, n + 1)
                nc.scalar.copy(part[:, :].rearrange("p (a n) -> p a n", a=2), halves(pT)[:, :, P:2 * P]).then_inc(part_ready, 1)
                act.wait_ge(kv_ready, n + 1)
                for h in range(2):
                    s = slice(h * HD, (h + 1) * HD)
                    i = nc.scalar.copy(bd_hi[s, s], kvT[s, s])
                i.then_inc(kv_hi_ready, 1)

            def act_m(n):
                act.wait_ge(m_put, n + 1)
                nc.scalar.copy(m_hi[:, ds(n * D, D)], m_bank(n)).then_inc(m_hi_ready, 1)

            def at_ready(c):
                act.wait_ge(kacc_done, c * NT)
                act.wait_ge(at_act, c)
                act.wait_ge(at_dve, c)

            def act_steps(c, j, last):
                for i in range(4):
                    n = c * NT + 4 * j + i
                    split_k(n, i % 2)
                    split_xnT(n + 2, (i - 2 if last and i >= 2 else 4 * j + (i + 2)), i % 2)
                    if not (isinstance(n, int) and n == NC * NT - 1):
                        split_xn(n + 1, (0 if last and i == 3 else 4 * j + (i + 1)), 1 - i % 2)
                    if isinstance(c, int) and (j, i) in WQ_SPLIT:
                        if (j, i) == WQ_SPLIT[0]:
                            act.wait_ge(xnT_stored, 64)
                            act.wait_ge(xn_lo_ready, n - 3)
                            act.wait_ge(xnT_lo_ready, n - 3)
                        half_wq(*divmod(WQ_SPLIT.index((j, i)), 2))
                    pair = 4 * (c - 1) + j
                    if i == 0:
                        act_operands(pair, j % 2, 32 * (2 * (c - 1) + j // 2) + 32)
                        act_pair(pair, j)
                    if i == 2:
                        act_kv(pair)
                    if i == 3:
                        act_m(pair)

            def half_wq(c, h):
                act.wait_ge(s_wq[c], 16)
                s = slice(h * 2 * CW, (h + 1) * 2 * CW)
                nc.scalar.copy(wq_hi[c][:, s], wk_in[:, s]).then_inc(wq_hi_ready, 1)

            with act.Fori(1, NC - 1) as c:
                at_ready(c)
                for j in range(4):
                    act_steps(c, j, j == 3)
                put_at(c)
            at_ready(NC - 1)
            for j in range(4):
                act_steps(NC - 1, j, j == 3)
            act_operands(NP - 4, 0, 32 * (NP // 2 - 2) + 32)
            put_at(NC - 1)
            at_ready(NC)

            def act_q(m, c, first):
                act.wait_ge(q_put, m + 1)
                if not (first and c < 2):
                    act.wait_ge(qs_ready, m - 1)
                nc.scalar.activation(q[:, (c % 2) * CW:(c % 2 + 1) * CW], pK[:, (c % 2) * 512:(c % 2 + 1) * 512],
                                     ACT.Relu).then_inc(q_ready, 1)

            def act_qsT(m, b):
                act.wait_ge(qsT_put, m + 1)
                if not (isinstance(m, int) and m < 2):
                    act.wait_ge(o_put, m - 1)
                nc.scalar.copy(qsT_hi[:, b * CW:(b + 1) * CW], pA[:, (2 + b) * 512:(3 + b) * 512]).then_inc(qsT_hi_ready, 1)

            def act_qx(t, b):
                act.wait_ge(q_put, 4 * t - 4)
                act.wait_ge(s_xnTin, 16 * t - 16)
                nc.scalar.copy(xnT_hi[:, b * D:(b + 1) * D], xnT_in[:, :]).then_inc(xnT_hi_ready, 1)

            def put_q(c):
                act_q(c, c, True)

            def put_qsT(c):
                act_qsT(c, c % 2)

            def wq_chunk(c):
                for h in range(2):
                    half_wq(c, h)

            def put_pair(n):
                if n > NP - 4:
                    act_operands(n, n % 2, 32 * (n // 2) + 32)
                act_pair(n, n % 4)

            start_q(lambda c: None, put_pair, act_kv, act_m, put_q, put_qsT,
                    wq_chunk, lambda c: None)

            def act_tile(t, b):
                for c in range(NC):
                    m = 4 * t + c
                    act_q(m, c, False)
                    if c == 0 and not (isinstance(t, int) and t == NT - 1):
                        act_qx(t + 1, 1 - b)
                    act_qsT(m - 1, (c - 1) % 2)
                    if c == 2:
                        sqrt_var(NT + t - 1)

            act_tile(1, 1)
            act.wait_ge(s_gw, 32)
            for n in range(3):
                i = nc.scalar.copy(gw_bank[n], gw_late[:, n * D:(n + 1) * D])
            i.then_inc(gw_put, 1)
            with act.Fori(1, NT // 2 - 1) as h:
                for b in range(2):
                    act_tile(2 * h + b, b)
            act_tile(NT - 2, 0)
            act_tile(NT - 1, 1)
            act_qsT(4 * NT - 1, 1)
            sqrt_var(2 * NT - 1)

            def w_hi(k):
                act.wait_ge(w_put, k + 1)
                src, rows, dst = w_step(k, w1_hi, w2_hi, w_bank(k))
                nc.scalar.copy(dst, src).then_inc(w_hi_ready, 1)
                if k in POOL_STEPS:
                    p = POOL_STEPS.index(k)
                    if p >= 4:
                        act.wait_ge(w_pool_ready, p - 3 if k < W1T else p - 1)
                    src, rows, _ = w_step(k, w1_hi, w2_hi, w_bank(k))
                    copy = raw(k)[:, :].rearrange("p (f n) -> p f n", f=FB) if k < W1T else raw(k)[0:rows]
                    nc.scalar.copy(copy, src).then_inc(w_raw_ready, 1)

            act.wait_ge(o_put, NC * NT)
            for k in range(6):
                w_hi(k)
            act.wait_ge(gap_ready, 1)
            nc.scalar.activation(ch[:, 16:32], ch[:, 0:16], ACT.Exp).then_inc(exp_ready, 1)
            def w_act_lo(k):
                act.wait_ge(w_sub_put, k - PE_STEPS[0] + 1)
                src, rows, dst = w_step(k, w1_lo, w2_lo, lo_bank(k))
                nc.scalar.copy(dst, src).then_inc(w_act_ready, 1)

            for k in range(6, 14):
                w_hi(k)
            for k in PE_STEPS:
                w_act_lo(k)
                if k + 2 in PE_STEPS:
                    w_hi(k + 2)
            act.wait_ge(row_hot_used, 32)
            nc.scalar.copy(table[:, :], pX[:, 0:3 * TW]).then_inc(table_ready, 1)
            for k in range(W1T, WSTEPS):
                w_hi(k)

            def act_gT(i):
                act.wait_ge(gT_put, i + 1)
                if not (isinstance(i, int) and i == 0):
                    act.wait_ge(h_put, i)
                nc.scalar.copy(gT_hi[:, :], pT[:, :]).then_inc(gT_hi_ready, 1)

            def act_h(i):
                act.wait_ge(h_put, i + 1)
                if not (isinstance(i, int) and i == 0):
                    act.wait_ge(hT_put, i)
                nc.scalar.copy(h_in[:, :], pK[:, 0:H]).then_inc(h_ready, 1)

            def act_silu(i, e):
                act.wait_ge(hT_put, i + 1)
                if not (isinstance(i, int) and i == 0):
                    act.wait_ge(hT_lo_ready, i)
                for b in range(HB):
                    w = min(P, H - b * P)
                    last = nc.scalar.activation(hT[0:w, b * P:(b + 1) * P], pX[0:w, b * P:(b + 1) * P], ACT.Silu,
                                                bias=b1T[0:w, ds(b * E + e, 1)])
                last.then_inc(hT_ready, 1)

            def act_tile_e(i, e=None, last=False):
                act_h(i)
                if not last:
                    act_gT(i + 1)
                if e is None:
                    e = act.value_load(tile_expert[0:1, ds(i, 1)], min_val=0, max_val=E - 1)
                act_silu(i, e)

            act.wait_ge(slots_ready, 1)
            first_expert = act.value_load(tile_expert[0:1, 0:1], min_val=0, max_val=E - 1)
            act.wait_ge(hT_ones, 1)
            nc.scalar.activation(warm[:, :], eps[:, :], ACT.Silu)
            act.wait_ge(w_put, WSTEPS)
            act_gT(0)
            act_tile_e(0, first_expert)
            with act.Fori(1, NS - 1) as i:
                act_tile_e(i)
            act_tile_e(NS - 1, last=True)

        @block.vector
        def _(dve):
            def newton_rstd(n):
                dve.wait_ge(sqrt_ready, n + 1)
                nc.vector.reciprocal(rs[:, 1:2], rs[:, 0:1]).then_inc(rstd_step, 1)
                dve.wait_ge(rstd_step, 4 * n + 1)
                nc.vector.tensor_scalar(rs[:, 2:3], mv[:, 1:2], EPS, rs[:, 1:2], ALU.add, ALU.mult).then_inc(rstd_step, 1)
                dve.wait_ge(rstd_step, 4 * n + 2)
                nc.vector.tensor_scalar(rs[:, 3:4], rs[:, 2:3], rs[:, 1:2], -0.5, ALU.mult, ALU.mult).then_inc(rstd_step, 1)
                dve.wait_ge(rstd_step, 4 * n + 3)
                nc.vector.tensor_scalar(rs[:, 4:5], rs[:, 3:4], 1.5, rs[:, 1:2], ALU.add, ALU.mult).then_inc(rstd_step, 1)
                dve.wait_ge(rstd_step, 4 * n + 4)

            def stats(src, n):
                nc.vector.bn_stats(st6[:, :], src).then_inc(bn_stats_done, 1)
                dve.wait_ge(bn_stats_done, n + 1)
                dve.nop(nofuse=True)
                nc.vector.bn_aggr(mv[:, :], st6[:, :]).then_inc(var_ready, 1)

            def normalize(dst, src):
                return nc.vector.tensor_scalar(dst, src, mv[:, 0:1], rs[:, 4:5], ALU.subtract, ALU.mult)

            def layernorm1(t, b):
                stats(xn[:, ds(t * D, D)], t)
                newton_rstd(t)
                if not (isinstance(t, int) and t < 2):
                    dve.wait_ge(xnT_put, t - 1)
                    dve.wait_ge(xn_kept, t - 1)
                normalize(xn_new[:, b * D:(b + 1) * D], xn[:, ds(t * D, D)]).then_inc(xn_ready, 1)

            def lo(dst, src, hi):
                return nc.vector.tensor_tensor(dst, src, f(hi), ALU.subtract)

            def split_wk(c):
                dve.wait_ge(wk_hi_ready, c + 1)
                for b in range(FB):
                    s = slice((c * FB + b) * CW, (c * FB + b + 1) * CW)
                    i = lo(wk_lo[:, s], wk_in[:, b * CW:(b + 1) * CW], wk_hi[:, s])
                i.then_inc(wk_lo_ready, 1)

            def split_xnT(n, t, b):
                dve.wait_ge(xnT_hi_ready, n + 1)
                s = slice(b * D, (b + 1) * D)
                lo(xnT_lo[:, s], xnT[:, ds(t * D, D)], xnT_hi[:, s]).then_inc(xnT_lo_ready, 1)

            def split_xn(n, t, b):
                dve.wait_ge(xn_hi_ready, n + 1)
                s = slice(b * D, (b + 1) * D)
                lo(xn_lo[:, s], xn[:, ds(t * D, D)], xn_hi[:, s]).then_inc(xn_lo_ready, 1)

            def split_k(n, b):
                dve.wait_ge(k_hi_ready, n + 1)
                s = slice(b * CW, (b + 1) * CW)
                nc.vector.scalar_tensor_tensor(out=k_lo[:, s], in0=pK[:, b * 512:(b + 1) * 512], scalar=0.0,
                                               in1=f(k_hi[:, s]), op0=ALU.max, op1=ALU.subtract
                                               ).then_inc(k_lo_ready, 1)

            def put_at(c):
                dve.wait_ge(a_done, c * NT + NT)
                for b in range(2, 4):
                    i = nc.vector.tensor_copy(at[:, b * CW:(b + 1) * CW], pA[:, b * 512:(b + 1) * 512])
                i.then_inc(at_dve, 1)

            dve.wait_ge(s_first, 16)
            layernorm1(0, 0)
            dve.wait_ge(s_x[0], 48)
            layernorm1(1, 1)
            split_wk(0)
            for t in range(2):
                split_xnT(t, t, t)
                layernorm1(t + 2, t)
            split_xn(0, 0, 0)

            def chunk0_pair(p):
                for b in range(2):
                    n = 2 * p + b
                    if not isinstance(p, int) or p < 6:
                        layernorm1(n + 4, b)
                    split_k(n, b)
                    split_xnT(n + 2, n + 2 if not isinstance(p, int) else (n + 2) % NT, b)
                    split_xn(n + 1, n + 1 if not isinstance(p, int) else (n + 1) % NT, 1 - b)

            dve.wait_ge(s_x[1], 64)
            chunk0_pair(0)
            dve.wait_ge(s_x[2], 64)
            dve.wait_ge(s_x[3], 64)
            with dve.Fori(1, 6) as p:
                chunk0_pair(p)
            split_wk(1)
            chunk0_pair(6)
            split_wk(2)
            chunk0_pair(7)
            put_at(0)
            split_wk(3)

            def dve_pair(n, j, b):
                dve.wait_ge(c_hi_ready, n + 1)
                if not (isinstance(n, int) and n >= NP - 4):
                    lo(wv_lo[:, :], wv_in[:, b * D:(b + 1) * D], wv_hi[:, :])
                    lo(wo_lo[:, :], wo_in[:, b * D:(b + 1) * D], wo_hi[:, :])
                nc.vector.tensor_tensor(blocks(at_hl)[:, :, P:2 * P], blocks(at)[:, :, j * P:(j + 1) * P],
                                        f(blocks(at_hl)[:, :, 0:P]), ALU.subtract)
                lo(ks_hl[:, P:2 * P], kacc[:, ds(n * P, P)], ks_hl[:, 0:P]).then_inc(c_lo_ready, 1)

            def dve_kv(n):
                dve.wait_ge(part_ready, n + 1)
                nc.vector.tensor_tensor(ksum[:, ds(n * P, P)], pT[:, 256:256 + P], part[:, P:2 * P], ALU.add)
                nc.vector.tensor_tensor(kvT[:, :], pT[:, 0:P], part[:, 0:P], ALU.add).then_inc(kv_ready, 1)
                dve.wait_ge(kv_hi_ready, n + 1)
                for h in range(2):
                    s = slice(h * HD, (h + 1) * HD)
                    i = lo(bd_lo[s, s], kvT[s, s], bd_hi[s, s])
                i.then_inc(kv_lo_ready, 1)

            def dve_m(n):
                dve.wait_ge(m_hi_ready, n + 1)
                lo(m_lo[:, ds(n * D, D)], m_bank(n), m_hi[:, ds(n * D, D)]).then_inc(m_lo_ready, 1)

            def half_wq(c, h):
                dve.wait_ge(wq_hi_ready, 2 * c + h + 1)
                s = slice(h * 2 * CW, (h + 1) * 2 * CW)
                lo(wq_lo[c][:, s], wk_in[:, s], wq_hi[c][:, s]).then_inc(wq_lo_ready, 1)

            def dve_chunk(c):
                for j in range(4):
                    for i in range(4):
                        n = c * NT + (4 * j + i)
                        split_k(n, i % 2)
                        split_xnT(n + 2, (4 * j + i + 2) % NT, i % 2)
                        if not (isinstance(n, int) and n == NC * NT - 1):
                            split_xn(n + 1, (4 * j + i + 1) % NT, 1 - i % 2)
                        if isinstance(c, int) and (j, i) in WQ_SPLIT:
                            half_wq(*divmod(WQ_SPLIT.index((j, i)), 2))
                        pair = 4 * c + (j - 4)
                        if i == 0:
                            dve_pair(pair, j, j % 2)
                        if i == 2:
                            dve_kv(pair)
                        if i == 3:
                            dve_m(pair)
                put_at(c)

            with dve.Fori(1, NC - 1) as c:
                dve_chunk(c)
            dve_chunk(NC - 1)

            heads = lambda a: a.rearrange("p (h d) -> p h d", h=HC)

            def dve_q(m, c):
                b = c % 2
                if not (isinstance(m, int) and m < 2):
                    dve.wait_ge(qsT_put, m - 1)
                dve.wait_ge(q_ready, m + 1)
                nc.vector.tensor_tensor(qs[:, b * CW:(b + 1) * CW], q[:, b * CW:(b + 1) * CW], ksum[:, c * CW:(c + 1) * CW],
                                        ALU.mult).then_inc(qk_ready, 1)
                dve.wait_ge(qk_ready, m + 1)
                nc.vector.tensor_reduce(nrm[:, 0:HC], heads(qs[:, b * CW:(b + 1) * CW]), AX_X, ALU.add).then_inc(nsum_ready, 1)
                dve.wait_ge(nsum_ready, m + 1)
                nc.vector.tensor_scalar(nrm[:, HC:2 * HC], nrm[:, 0:HC], 1e-6, None, ALU.max).then_inc(nclip_ready, 1)
                dve.wait_ge(nclip_ready, m + 1)
                nc.vector.reciprocal(nrm[:, 2 * HC:3 * HC], nrm[:, HC:2 * HC]).then_inc(nrec_ready, 1)
                dve.wait_ge(nrec_ready, m + 1)
                nc.vector.tensor_tensor(heads(qs[:, b * CW:(b + 1) * CW]), heads(q[:, b * CW:(b + 1) * CW]),
                                        nrm[:, 2 * HC:3 * HC].unsqueeze(2).to_broadcast([P, HC, HD]),
                                        ALU.mult).then_inc(qs_ready, 1)

            def dve_qsT(m, b):
                dve.wait_ge(qsT_hi_ready, m + 1)
                s = slice(b * CW, (b + 1) * CW)
                lo(qsT_lo[:, s], pA[:, (2 + b) * 512:(3 + b) * 512], qsT_hi[:, s]).then_inc(qsT_lo_ready, 1)

            def dve_qx(t, b):
                dve.wait_ge(xnT_hi_ready, t + (NC * NT + 1))
                s = slice(b * D, (b + 1) * D)
                lo(xnT_lo[:, s], xnT_in[:, :], xnT_hi[:, s]).then_inc(xnT_lo_ready, 1)

            def residual(t):
                dve.wait_ge(o_put, 4 * t + 4)
                dve.wait_ge(xb_ready, t + 1)
                if not (isinstance(t, int) and t == 0):
                    dve.wait_ge(x2_stored, 16 * t)
                nc.vector.tensor_tensor(x2[:, :], pX[:, :], xb[:, :], ALU.add).then_inc(x2_ready, 1)

            def layernorm2(t):
                newton_rstd(NT + t)
                if not (isinstance(t, int) and t == 0):
                    dve.wait_ge(xn2_stored, 16 * t)
                normalize(xn2[:, :], x2[:, :]).then_inc(xn2_ready, 1)

            def dots(t, first, last):
                dve.wait_ge(xn2_ready, t + 1)
                for e in range(first, last):
                    w = gw_b[:, e * D:(e + 1) * D] if e < 5 else gw_bank[e - 5]
                    if not (isinstance(t, int) and t == 0 and e < 2):
                        dve.wait_ge(dots_done, E * t + (e - 1))
                    nc.vector.scalar_tensor_tensor(out=gprod[e % 2][:, :], in0=xn2[:, :], scalar=1.0, in1=w, op0=ALU.mult,
                                                   op1=ALU.mult, accum_out=scores[:, e:e + 1]).then_inc(dots_done, 1)

            def put_scores(t):
                dve.wait_ge(dots_done, E * t + E)
                s = scores[:, :]
                nc.vector.tensor_tensor(s, s, gb_b[:, :], ALU.add).then_inc(score_sum, 1)
                dve.wait_ge(score_sum, t + 1)
                nc.vector.tensor_tensor(s, s, gb2_b[:, :], ALU.add).then_inc(score_ready, 1)
                dve.wait_ge(score_ready, t + 1)
                dve.nop(nofuse=True)
                nc.vector.max(top8[:, :], s).then_inc(top_done, 1)
                dve.wait_ge(top_done, t + 1)
                dve.nop(nofuse=True)
                nc.vector.max_index(topi8[:, :], top8[:, :], s).then_inc(topi_done, 1)
                nc.vector.tensor_copy(top[:, ds(t * E, E)], top8[:, :])
                dve.wait_ge(topi_done, t + 1)
                nc.vector.tensor_copy(topi[:, ds(t * E, E)], topi8[:, :]).then_inc(top_kept, 1)

            def wq_chunk(c):
                for h in range(2):
                    half_wq(c, h)

            start_q(lambda c: None, lambda n: dve_pair(n, n % 4, n % 2), dve_kv, dve_m, lambda c: dve_q(c, c),
                    lambda c: dve_qsT(c, c % 2), wq_chunk, lambda c: None)
            dve.wait_ge(s_small, 48)
            dve.wait_ge(kv_put, NP)
            nc.vector.tensor_scalar(neg_ident[:, :], ident[:, :], -1.0, None, ALU.mult).then_inc(neg_ready, 1)

            def dve_tile(t, b, first=False):
                for c in range(NC):
                    m = 4 * t + c
                    if c == 2:
                        residual(t - 1)
                        dve.wait_ge(x2_ready, t)
                        stats(x2[:, :], t + (NT - 1))
                        if not first:
                            put_scores(t - 2)
                    dve_qsT(m - 1, (c - 1) % 2)
                    dve_q(m, c)
                    if c == 0 and not (isinstance(t, int) and t == NT - 1):
                        dve_qx(t + 1, 1 - b)
                    if c == 2:
                        layernorm2(t - 1)
                    if first and c == 3:
                        dve.wait_ge(s_gw, 32)
                    if c == 3:
                        dots(t - 1, 0, 4)
                    if c == 0 and not first:
                        dots(t - 2, 4, E)

            dve_tile(1, 1, True)
            dve.wait_ge(gw_put, 1)
            with dve.Fori(1, NT // 2 - 1) as h:
                for b in range(2):
                    dve_tile(2 * h + b, b)
            dve_tile(NT - 2, 0)
            dve_tile(NT - 1, 1)
            dve_qsT(4 * NT - 1, 1)
            dots(NT - 2, 4, E)
            residual(NT - 1)
            dve.wait_ge(x2_ready, NT)
            stats(x2[:, :], 2 * NT - 1)
            put_scores(NT - 2)
            layernorm2(NT - 1)
            dots(NT - 1, 0, E)
            put_scores(NT - 1)

            linked = [0]

            def link(ins):
                linked[0] += 1
                ins.then_inc(r_chain, 1)
                dve.wait_ge(r_chain, linked[0])

            def w_lo(k):
                if k == W1T:
                    dve.wait_ge(w_pool_ready, first_late)
                if k not in DVE_STEPS:
                    return
                dve.wait_ge(w_hi_ready, k + 1)
                src, rows, dst = w_step(k, w1_lo, w2_lo, w_bank(k))
                hi = w_step(k, w1_hi, w2_hi, w_bank(k))[2]
                nc.vector.tensor_tensor(dst, src, f(hi), ALU.subtract).then_inc(w_lo_ready, 1)

            v = nc.vector
            many = lambda a, n: a.unsqueeze(1).to_broadcast([P, n, a.shape[1]])
            by8 = lambda a: a.rearrange("p (n e) -> p n e", e=E)
            top3, topi3 = by8(top[:, :]), by8(topi[:, :])
            dve.wait_ge(top_kept, NT)
            v.tensor_tensor(ch[:, 0:16], top3[:, :, 1], top3[:, :, 0], ALU.subtract).then_inc(gap_ready, 1)
            for c in range(2):
                i = v.tensor_copy(row(1)[:, c * NT:(c + 1) * NT], topi3[:, :, c])
            link(i)
            dve.wait_ge(r_consts, 1)
            link(v.tensor_tensor(by8(hot[:, :]), wide(row(1), E), many(iota_e[:, :], 2 * NT), ALU.is_equal))
            v.memset(mask[:, NT * E:(NT + 1) * E], 0.0)
            v.tensor_tensor(mask[:, 0:NT * E], hot[:, 0:NT * E], hot[:, NT * E:2 * NT * E], ALU.add).then_inc(mask_ready, 1)
            dve.wait_ge(exp_ready, 1)
            link(v.tensor_scalar(ch[:, 0:16], ch[:, 16:32], 1.0, None, ALU.add))
            link(v.reciprocal(row(2)[:, 0:NT], ch[:, 0:16]))
            link(v.tensor_tensor(row(2)[:, NT:2 * NT], ch[:, 16:32], row(2)[:, 0:NT], ALU.mult))
            link(v.tensor_copy(gate_hl[:, 0:32], row(2)))
            link(lo(gate_hl[:, 32:64], row(2), gate_hl[:, 0:32]))
            dve.wait_ge(rank_put, 1)
            n_e = pT[:, NT * E:(NT + 1) * E]
            c16 = cmp[:, 0:E * NT].rearrange("p (e k) -> p e k", e=E)
            link(v.tensor_tensor(c16, wide(n_e, NT), many(k128[:, :], E), ALU.is_gt))
            link(v.tensor_reduce(small[:, 0:E], c16, AX_X, ALU.add))
            link(v.tensor_tensor(by8(cmp[:, 0:E * E]), by8(tri8[:, :]), many(small[:, 0:E], E), ALU.mult))
            link(v.tensor_reduce(small[:, E:2 * E], by8(cmp[:, 0:E * E]), AX_X, ALU.add))
            link(v.tensor_tensor(small[:, 2 * E:3 * E], small[:, E:2 * E], small[:, 0:E], ALU.subtract))
            link(v.tensor_scalar(small[:, 2 * E:3 * E], small[:, 2 * E:3 * E], float(P), None, ALU.mult))
            link(v.tensor_tensor(by8(slot_of[:, :]), by8(pT[:, 0:NT * E]), many(small[:, 2 * E:3 * E], NT), ALU.add))
            for c in range(2):
                i = v.tensor_tensor(prod[:, c * NT * E:(c + 1) * NT * E], hot[:, c * NT * E:(c + 1) * NT * E],
                                    slot_of[:, :], ALU.mult)
            link(i)
            link(v.tensor_reduce(row(3), by8(prod[:, :]), AX_X, ALU.add))
            link(v.tensor_copy(ch_i[:, 0:32], row(3)))
            v.tensor_scalar(ch_i[:, 32:64], ch_i[:, 0:32], P - 1, None, ALU.bitwise_and)
            link(v.tensor_scalar(ch_i[:, 64:96], ch_i[:, 0:32], 7, None, ALU.logical_shift_right))
            v.tensor_copy(row(4), ch_i[:, 32:64]).then_inc(rows_ready, 1)
            link(v.tensor_copy(row(5), ch_i[:, 64:96]))
            v.tensor_tensor(sv[:, :, 2, :], wide(row(5), TW), many(iota_j[:, :], 2 * NT), ALU.is_equal).then_inc(tile_hot_ready, 1)
            dve.wait_ge(tile_hot_ready, 1)
            link(v.tensor_tensor(sv[:, :, 1, :], th, wide(f(gate_hl[:, 0:32]), TW), ALU.mult))

            def put_row_hots(first, last):
                for a in range(first, last):
                    if a % 4 == 3:
                        continue
                    if a >= RH:
                        dve.wait_ge(row_hot_used, a - RH + 1)
                    v.tensor_scalar(row_hot(a), iota_r[:, :], row(4)[:, a:a + 1], None, ALU.is_equal).then_inc(row_hot_ready, 1)

            put_row_hots(0, RH)
            dve.wait_ge(tokens_ready, 1)
            v.tensor_tensor(sv[:, :, 2, :], th, wide(f(gate_hl[:, 32:64]), TW), ALU.mult).then_inc(vals_ready, 1)
            put_row_hots(RH, 2 * NT)
            link(v.tensor_tensor(by8(cmp[:, :]), many(small[:, E:2 * E], TW), wide(iota_j[:, :], E), ALU.is_le))
            link(v.tensor_reduce(padt[:, 0:TW], by8(cmp[:, :]), AX_X, ALU.add))
            link(v.tensor_scalar(tile_expert[:, :], padt[:, 0:TW], float(E - 1), None, ALU.min))
            dve.wait_ge(table_ready, 1)
            link(v.tensor_scalar(padt[:, 0:TW], table[:, 0:TW], 0.0, pad[:, :], ALU.is_equal, ALU.mult))
            v.tensor_tensor(slot_gate[:, :], table[:, TW:2 * TW], table[:, 2 * TW:3 * TW], ALU.add)
            v.scalar_tensor_tensor(out=slot_token[:, :], in0=table[:, 0:TW], scalar=-1.0, in1=padt[:, 0:TW],
                                   op0=ALU.add, op1=ALU.add).then_inc(slots_ready, 1)
            for k in range(W1T, WSTEPS):
                w_lo(k)

            dve.wait_ge(w_put, WSTEPS)
            link(v.memset(hT[96:128, 2 * P:3 * P], 0.0))
            v.memset(hT[96:97, 2 * P:3 * P], 1.0).then_inc(hT_ones, 1)

            def dve_gT(i):
                dve.wait_ge(gT_hi_ready, i + 1)
                lo(gT_lo[:, :], pT[:, :], gT_hi[:, :]).then_inc(gT_lo_ready, 1)

            def dve_hT(i):
                dve.wait_ge(hT_ready, i + 1)
                if not (isinstance(i, int) and i == 0):
                    dve.wait_ge(y_put, i)
                v.tensor_copy(hT_hi[:, :], hT[:, :]).then_inc(hT_hi_ready, 1)
                dve.wait_ge(hT_hi_ready, i + 1)
                lo(hT_lo[:, :], hT[:, :], hT_hi[:, :]).then_inc(hT_lo_ready, 1)

            def dve_y(i, b):
                dve.wait_ge(y_put, i + 1)
                if not (isinstance(i, int) and i < 2):
                    dve.wait_ge(sidx_ready, i)
                v.tensor_scalar(y[:, b * D:(b + 1) * D], pK[:, 512:1024], slot_gate[:, ds(i, 1)], None,
                                ALU.mult).then_inc(y_ready, 1)

            dve_gT(0)
            dve_gT(1)
            dve_hT(0)
            dve_gT(2)
            dve_y(0, 0)
            dve_hT(1)
            with dve.Fori(1, NS // 2) as h:
                for b in range(2):
                    dve_gT(2 * h + (b + 1))
                    dve_y(2 * h + (b - 1), 1 - b)
                    dve_hT(2 * h + b)
            dve_y(NS - 2, 1)
            dve_hT(NS - 1)
            dve_y(NS - 1, 0)

        @block.tensor
        def _(pe):
            def three(dst, lhs, rhs, start, stop):
                nc.tensor.matmul(dst, lhs[0], rhs[0], start=start, stop=False)
                nc.tensor.matmul(dst, lhs[0], rhs[1], start=False, stop=False)
                return nc.tensor.matmul(dst, lhs[1], rhs[0], start=False, stop=stop)

            def two(pair, at, n):
                return (pair[0][:, at:at + n] if isinstance(at, int) else pair[0][:, ds(at, n)],
                        pair[1][:, at:at + n] if isinstance(at, int) else pair[1][:, ds(at, n)])

            pe.wait_ge(ident_ready, 1)
            def transpose_xn(t, b):
                pe.wait_ge(xn_ready, t + 1)
                if not (isinstance(t, int) and t == 0):
                    pe.wait_ge(xnT_ready, t)
                for i in range(FB):
                    last = nc.tensor.transpose(pT[:, i * P:(i + 1) * P], xn_new[:, b * D + i * P:b * D + (i + 1) * P], ident[:, :])
                last.then_inc(xnT_put, 1)

            def project_k(n, c, b):
                pe.wait_ge(xnT_lo_ready, n + 1)
                if not (isinstance(n, int) and n < 2):
                    pe.wait_ge(k_lo_ready, n - 1)
                for i in range(FB):
                    last = three(pK[:, b * 512:(b + 1) * 512], two((xnT_hi, xnT_lo), b * D + i * P, P),
                                 two((wk_hi, wk_lo), c * (FB * CW) + i * CW, CW), i == 0, i == FB - 1)
                last.then_inc(kproj_done, 1)

            def accumulate_at(n, b, start=False, stop=False):
                pe.wait_ge(xn_lo_ready, n + 1)
                pe.wait_ge(k_lo_ready, n + 1)
                for i in range(FB):
                    last = three(pA[:, i * 512:(i + 1) * 512], two((xn_hi, xn_lo), b * D + i * P, P),
                                 two((k_hi, k_lo), b * CW, CW), start, stop)
                last.then_inc(a_done, 1)

            for t in range(2):
                transpose_xn(t, t)
            pe.wait_ge(s_b, 32)
            for b in range(HB):
                w = min(P, H - b * P)
                nc.tensor.transpose(pX[0:w, 32 + b * E:32 + (b + 1) * E], b1_in[:, b * P:b * P + w], ident[0:E, 0:E])
            nc.tensor.transpose(pX[:, 64:96], b2_in[:, :], ident[0:32, 0:32]).then_inc(bT_put, 1)
            pe.wait_ge(wk_lo_ready, 1)
            project_k(0, 0, 0)

            def chunk0_pair(p):
                for b in range(2):
                    n = 2 * p + b
                    if not isinstance(p, int) or p < 7:
                        transpose_xn(n + 2, b)
                    if not isinstance(n, int) or n < NT - 1:
                        project_k(n + 1, 0, 1 - b)
                    accumulate_at(n, b, isinstance(n, int) and n == 0, isinstance(n, int) and n == NT - 1)

            chunk0_pair(0)
            with pe.Fori(1, 7) as p:
                chunk0_pair(p)
            chunk0_pair(7)

            def pe_kv(n):
                if isinstance(n, int) and n >= NP - 4:
                    pe.wait_ge(operands_lo, n - (NP - 4) + 1)
                pe.wait_ge(c_lo_ready, n + 1)
                for i in range(FB):
                    for w in (wv_hi, wv_lo):
                        nc.tensor.matmul(pT[:, 0:256], w[:, i * P:(i + 1) * P], at_hl[:, i * 256:(i + 1) * 256],
                                         start=i == 0 and w is wv_hi, stop=i == FB - 1 and w is wv_lo)
                nc.tensor.matmul(pT[:, 256:512], ones[:, :], ks_hl[:, :], start=True, stop=True).then_inc(kv_put, 1)

            def pe_m(n):
                pe.wait_ge(kv_lo_ready, n + 1)
                three(m_bank(n), (bd_hi[:, :], bd_lo[:, :]), (wo_hi[:, :], wo_lo[:, :]), True, True).then_inc(m_put, 1)

            def pe_chunk(c):
                n0 = c * NT
                pe.wait_ge(wk_lo_ready, c + 1)
                project_k(n0, c, 0)
                for j in range(4):
                    for i in range(4):
                        n = n0 + (4 * j + i)
                        if 4 * j + i < NT - 1:
                            project_k(n + 1, c, 1 - i % 2)
                        if j == 0 and i == 0:
                            pe.wait_ge(at_act, c)
                            pe.wait_ge(at_dve, c)
                        accumulate_at(n, i % 2, j == 0 and i == 0, j == 3 and i == 3)
                        if i == 1:
                            pe_kv(4 * c + (j - 4))
                        if i == 2:
                            pe_m(4 * c + (j - 4))

            with pe.Fori(1, NC - 1) as c:
                pe_chunk(c)
            pe_chunk(NC - 1)

            def project_q(m, t, c, b):
                if c == 0:
                    pe.wait_ge(xnT_lo_ready, t + (NC * NT + 1))
                if isinstance(m, int) and m < NC:
                    pe.wait_ge(wq_lo_ready, 2 * c + 2)
                if not (isinstance(m, int) and m < 2):
                    pe.wait_ge(q_ready, m - 1)
                for i in range(FB):
                    last = three(pK[:, (c % 2) * 512:(c % 2 + 1) * 512], two((xnT_hi, xnT_lo), b * D + i * P, P),
                                 two((wq_hi[c], wq_lo[c]), i * CW, CW), i == 0, i == FB - 1)
                last.then_inc(q_put, 1)

            def transpose_qs(m, b):
                pe.wait_ge(qs_ready, m + 1)
                if not (isinstance(m, int) and m < 2):
                    pe.wait_ge(qsT_lo_ready, m - 1)
                for j in range(CB):
                    i = nc.tensor.transpose(pA[:, (2 + b) * 512 + j * P:(2 + b) * 512 + (j + 1) * P],
                                            qs[:, b * CW + j * P:b * CW + (j + 1) * P], ident[:, :])
                i.then_inc(qsT_put, 1)

            def times_m(m, c):
                pe.wait_ge(qsT_lo_ready, m + 1)
                for j in range(CB):
                    last = three(pX[:, :], two((qsT_hi, qsT_lo), (c % 2) * CW + j * P, P),
                                 two((m_hi, m_lo), (c * CB + j) * D, D), c == 0 and j == 0, c == NC - 1 and j == CB - 1)
                last.then_inc(o_put, 1)

            start_q(lambda c: project_q(c, 0, c, 0), lambda n: None, pe_kv, pe_m, lambda c: None,
                    lambda c: transpose_qs(c, c % 2), lambda c: None, lambda c: times_m(c, c))

            def pe_tile(t, b):
                for c in range(NC):
                    m = 4 * t + c
                    project_q(m, t, c, b)
                    transpose_qs(m - 1, (c - 1) % 2)
                    if c == 2:
                        pe.wait_ge(x2_ready, t)
                    if isinstance(t, int) and t == 1 and c == 1:
                        pe.wait_ge(m_lo_ready, NP)
                    times_m(m - 2, (c - 2) % 4)

            pe_tile(1, 1)
            with pe.Fori(1, NT // 2) as h:
                for b in range(2):
                    pe_tile(2 * h + b, b)
            transpose_qs(4 * NT - 1, 1)
            times_m(4 * NT - 2, 2)
            times_m(4 * NT - 1, 3)

            def w_transpose(k):
                if k == 0:
                    pe.wait_ge(s_w1a, 16 * 7)
                    pe.wait_ge(qsT_lo_ready, NC * NT)
                if k == 7:
                    pe.wait_ge(s_w1b, 16 * 9)
                if k == 16:
                    pe.wait_ge(s_w1c, 16 * 6)
                if k - 4 in POOL_STEPS:
                    pe.wait_ge(w_raw_ready, POOL_STEPS.index(k - 4) + 1)
                elif k - 4 in PE_STEPS:
                    pe.wait_ge(w_hi_ready, k - 3)
                elif k - 4 in DVE_STEPS:
                    pe.wait_ge(w_lo_ready, DVE_STEPS.index(k - 4) + 1)
                bank = w_bank(k)
                if k < W1T:
                    for b in range(FB):
                        i = nc.tensor.transpose(bank[:, b * P:(b + 1) * P],
                                                w1_in[k][:, b * P:(b + 1) * P], ident[:, :])
                else:
                    e, hb = divmod(k - W1T, HB)
                    if hb == 0:
                        pe.wait_ge(s_w2[e], 16)
                        pe.wait_ge(b2_put, e + 1)
                    w = min(P, W2C - hb * P)
                    for b in range(FB):
                        i = nc.tensor.transpose(bank[0:w, b * P:(b + 1) * P],
                                                w2_in[e][:, b * W2C + hb * P:b * W2C + hb * P + w], ident[:, :])
                i.then_inc(w_put, 1)

            for k in range(8):
                w_transpose(k)
            pe.wait_ge(mask_ready, 1)
            pe.wait_ge(r_consts, 1)
            nc.tensor.matmul(pT[:, 0:(NT + 1) * E], before[:, :], mask[:, :], start=True, stop=False)
            for t in range(NT):
                n = NT - t
                i = nc.tensor.matmul(pT[:, (t + 1) * E:(NT + 1) * E].rearrange("p (n e) -> p n e", e=E), ones_b[:, :],
                                     mask[:, t * E:(t + 1) * E].unsqueeze(1).to_broadcast([P, n, E]),
                                     start=False, stop=t == NT - 1)
            i.then_inc(rank_put, 1)
            def subtract_hi(k):
                if k - 2 in PE_STEPS:
                    pe.wait_ge(w_act_ready, k - 2 - PE_STEPS[0] + 1)
                for b in range(FB):
                    nc.tensor.matmul(lo_bank(k)[:, b * P:(b + 1) * P], w1_in[k][:, b * P:(b + 1) * P], ident[:, :],
                                     is_transpose=True, start=b == 0, stop=False)
                pe.wait_ge(w_hi_ready, k + 1)
                hi = w_step(k, w1_hi, w2_hi, w_bank(k))[2]
                nc.tensor.matmul(lo_bank(k).rearrange("p (f n) -> p f n", f=FB), neg_ident[:, :], hi,
                                 start=False, stop=True).then_inc(w_sub_put, 1)

            for k in range(8, 14):
                w_transpose(k)
            pe.wait_ge(neg_ready, 1)
            for k in PE_STEPS:
                subtract_hi(k)
                if k + 2 in PE_STEPS:
                    w_transpose(k + 2)
            pe.wait_ge(vals_ready, 1)
            for a in range(2 * NT):
                pe.wait_ge(row_hot2_ready if a % 4 == 3 else row_hot_ready, a // 4 + 1 if a % 4 == 3 else a - a // 4 + 1)
                nc.tensor.matmul(pX[:, 0:3 * TW], row_hot(a), slot_val[:, a * 3 * TW:(a + 1) * 3 * TW], start=a == 0,
                                 stop=a == 2 * NT - 1).then_inc(row_hot_used, 1)
            def pe_gT(i, b):
                pe.wait_ge(s_g[b], 16 * (i // 2) + 16 if isinstance(i, int) else 8 * i + (16 - 8 * b))
                if not (isinstance(i, int) and i == 0):
                    pe.wait_ge(gT_lo_ready, i)
                for n in range(FB):
                    last = nc.tensor.transpose(pT[:, n * P:(n + 1) * P], xg[:, b * D + n * P:b * D + (n + 1) * P], ident[:, :])
                last.then_inc(gT_put, 1)

            def pe_h(i, e):
                pe.wait_ge(gT_lo_ready, i + 1)
                if not (isinstance(i, int) and i == 0):
                    pe.wait_ge(h_ready, i)
                for n in range(FB):
                    last = three(pK[:, 0:H], two((gT_hi, gT_lo), n * P, P), two((w1_hi, w1_lo), e * H + n * EH, H),
                                 n == 0, n == FB - 1)
                last.then_inc(h_put, 1)

            def pe_hT(i):
                pe.wait_ge(h_ready, i + 1)
                if not (isinstance(i, int) and i == 0):
                    pe.wait_ge(hT_ready, i)
                for n in range(HB):
                    w = min(P, H - n * P)
                    last = nc.tensor.transpose(pX[0:w, n * P:(n + 1) * P], h_in[:, n * P:n * P + w], ident[:, :])
                last.then_inc(hT_put, 1)

            def pe_y(i, e):
                pe.wait_ge(hT_lo_ready, i + 1)
                if not (isinstance(i, int) and i == 0):
                    pe.wait_ge(y_ready, i)
                for n in range(HB):
                    w = min(P, W2C - n * P)
                    hs = (hT_hi[0:w, n * P:(n + 1) * P], hT_lo[0:w, n * P:(n + 1) * P])
                    at_ = e * (HB * D) + n * D
                    last = three(pK[:, 512:1024], hs, (w2_hi[0:w, ds(at_, D)], w2_lo[0:w, ds(at_, D)]),
                                 n == 0, n == HB - 1)
                last.then_inc(y_put, 1)

            def expert(i):
                return pe.value_load(tile_expert[0:1, ds(i, 1)], min_val=0, max_val=E - 1)

            for k in range(W1T, 28):
                w_transpose(k)
            pe.wait_ge(slots_ready, 1)
            first_experts = [expert(i) for i in range(2)]
            for k in range(28, WSTEPS - 4):
                w_transpose(k)
            pe_gT(0, 0)
            for k in range(WSTEPS - 4, WSTEPS):
                w_transpose(k)

            pe.wait_ge(w_lo_ready, len(DVE_STEPS))
            pe.wait_ge(w_act_ready, len(PE_STEPS))
            pe.wait_ge(w_pool_ready, len(POOL_STEPS))
            pe_h(0, first_experts[0])
            pe_gT(1, 1)
            pe_hT(0)
            pe_h(1, first_experts[1])
            pe_gT(2, 0)
            pe_y(0, first_experts[0])
            pe_hT(1)
            with pe.Fori(1, NS // 2) as h:
                for b in range(2):
                    i = 2 * h + b
                    pe_h(i, expert(i))
                    pe_gT(2 * h + (b + 1), 1 - b)
                    pe_y(2 * h + (b - 1), expert(2 * h + (b - 1)))
                    pe_hT(i)
            pe_h(NS - 1, expert(NS - 1))
            pe_y(NS - 2, expert(NS - 2))
            pe_hT(NS - 1)
            pe_y(NS - 1, expert(NS - 1))


_NAMES = ["attn_hidden_states", "attn_Wq", "attn_Wk", "attn_Wv", "attn_Wo", "attn_bo",
          "ffn_gate_w", "ffn_gate_b", "ffn_bias", "ffn_w1", "ffn_b1", "ffn_w2", "ffn_b2"]


def kernel(**inputs):
    import numpy as np
    import concourse.bacc as bacc
    from concourse.bass_utils import run_bass_kernel_spmd as _run

    nc = bacc.Bacc("TRN2", target_bir_lowering=False, num_devices=1)
    arrays, args = {}, []
    for name in _NAMES:
        a = np.ascontiguousarray(inputs["L0_" + name])
        if name == "attn_hidden_states":
            a = a.reshape(T, D)
        arrays[f"in_{name}"] = a
        args.append(nc.dram_tensor(f"in_{name}", a.shape, F32, kind="ExternalInput").ap())
    args.append(nc.dram_tensor("out", (T + P, D), F32, kind="ExternalOutput").ap())
    block_kernel(nc, *args)
    r = _run(nc, [arrays], core_ids=[0])
    return r.results[0]["out"][:T].reshape(1, T, D)
```
